# Optimizing a Trainium2 kernel written in Bass

```python
import numpy as np
import jax
import jax.numpy as jnp

def _softmax(x, axis=-1):
    return jax.nn.softmax(x, axis=axis)
def _gelu(x):
    return jax.nn.gelu(x, approximate=True)
def _silu(x):
    return jax.nn.silu(x)
def _sigmoid(x):
    return jax.nn.sigmoid(x)
def _layernorm(x, axis=-1, eps=1e-5):
    m = jnp.mean(x, axis=axis, keepdims=True)
    v = jnp.var(x, axis=axis, keepdims=True)
    return (x - m) / jnp.sqrt(v + eps)
def _scatter_add(tgt, idx, src, axis=0):
    return tgt.at[idx].add(src)
def _segment_sum(src, seg, n):
    return jax.ops.segment_sum(src, seg, n)

kernel_name = 'mk_audio_tower_d2_tok_audfeat256_9aa216'

def setup_inputs(seed: int = 0):
    np.random.seed(seed)
    _w = jnp.asarray
    def _rec_inputs():
        import jax
        import jax.numpy as jnp
        _rk = jax.random.key(seed)
        x = (-0.000520686 + 1.00062 * jax.random.normal(jax.random.fold_in(_rk, 1), (32, 1024, 256), jnp.float32))
        return x
    x = _rec_inputs()
    def _L0_tok_setup():
        import jax, jax.numpy as jnp
        import numpy as np
        BATCH = 2
        SEQ = 4096
        D_MODEL = 256
        N_STATE = 64
        DT_RANK = 1
        NUM_LAYERS = 3

        def _ssm_layer(x, A_log, Dp, W_dbc, W_dt, b_dt):
            A = -jnp.exp(A_log)
            dbc = jnp.einsum('ble,ce->blc', x, W_dbc)
            delta, Bm, Cm = jnp.split(dbc, [DT_RANK, DT_RANK + N_STATE], axis=-1)
            delta = jax.nn.softplus(jnp.einsum('blr,er->ble', delta, W_dt) + b_dt)
            dA = jnp.exp(delta[..., None] * A)
            dBx = (delta * x)[..., None] * Bm[:, :, None, :]

            def combine(c1, c2):
                a1, h1 = c1
                a2, h2 = c2
                return (a1 * a2, h1 * a2 + h2)
            _, hs = jax.lax.associative_scan(combine, (dA, dBx), axis=1)
            y = jnp.einsum('blen,bln->ble', hs, Cm)
            return y + Dp * x
        key = jax.random.key(seed)
        kx, kw1, kw2 = jax.random.split(key, 3)
        x = jax.random.normal(kx, (BATCH, SEQ, D_MODEL), dtype=jnp.float32)
        A_log = jnp.broadcast_to(jnp.log(jnp.arange(1, N_STATE + 1, dtype=jnp.float32)), (NUM_LAYERS, D_MODEL, N_STATE)).copy()
        D = jnp.ones((NUM_LAYERS, D_MODEL), dtype=jnp.float32)
        W_dbc = 0.02 * jax.random.normal(kw1, (NUM_LAYERS, DT_RANK + 2 * N_STATE, D_MODEL), dtype=jnp.float32)
        W_dt = 0.02 * jax.random.normal(kw2, (NUM_LAYERS, D_MODEL, DT_RANK), dtype=jnp.float32)
        b_dt = jnp.zeros((NUM_LAYERS, D_MODEL), dtype=jnp.float32)
        return {'x': x, 'A_log': A_log, 'D': D, 'W_dbc': W_dbc, 'W_dt': W_dt, 'b_dt': b_dt}
    _L0_tok_all = _L0_tok_setup()
    _L0_tok_in = {k: v for k, v in _L0_tok_all.items() if k in ('A_log', 'D', 'W_dbc', 'W_dt', 'b_dt', )}
    del _L0_tok_all

    def _L0_attn_setup():
        import jax, jax.numpy as jnp
        import numpy as np
        B_SZ, L, H, P = (16, 1024, 256, 256)
        DT_MIN, DT_MAX = (0.001, 0.1)

        def _binop(ei, ej):
            ai, bi = ei
            aj, bj = ej
            return (aj * ai, aj * bi + bj)
        key = jax.random.key(seed)
        ks = jax.random.split(key, 6)
        u = jax.random.normal(ks[0], (B_SZ, L, H), dtype=jnp.float32)
        Lambda_re = -0.5 * jnp.ones((P,), jnp.float32)
        Lambda_im = jnp.pi * jnp.arange(P, dtype=jnp.float32)
        Bp = jax.random.normal(ks[1], (P, H, 2), jnp.float32) / jnp.sqrt(2.0 * H)
        Cp = jax.random.normal(ks[2], (H, P, 2), jnp.float32) / jnp.sqrt(2.0 * P)
        D = jax.random.normal(ks[3], (H,), jnp.float32)
        log_step = jax.random.uniform(ks[4], (P, 1), jnp.float32) * (jnp.log(DT_MAX) - jnp.log(DT_MIN)) + jnp.log(DT_MIN)
        return {'u': u, 'Lambda_re': Lambda_re, 'Lambda_im': Lambda_im, 'B': Bp, 'C': Cp, 'D': D, 'log_step': log_step}
    _L0_attn_all = _L0_attn_setup()
    _L0_attn_in = {k: v for k, v in _L0_attn_all.items() if k in ('Lambda_re', 'Lambda_im', 'B', 'C', 'D', 'log_step', )}
    del _L0_attn_all

    def _L0_ffn_setup():
        import jax, jax.numpy as jnp
        import numpy as np
        B, N, D = (16, 4096, 256)
        NUM_EXPERTS, TOP_K, HEADS = (4, 2, 4)
        N_EDGES = 1048576
        LN_EPS = 1e-05

        def _layernorm(x, g, b):
            mu = x.mean(-1, keepdims=True)
            var = ((x - mu) ** 2).mean(-1, keepdims=True)
            return (x - mu) * jax.lax.rsqrt(var + LN_EPS) * g + b

        def _forward(x, edge_index, W_gat, att_src, att_dst, b_gat, ln_gamma, ln_beta, W1, b1, W2, b2):
            Bc, Nc, Dc = x.shape
            M = Bc * Nc
            x_flat = x.reshape(M, Dc)
            h = (x_flat @ W_gat).reshape(M, HEADS, NUM_EXPERTS)
            loops = jnp.arange(M, dtype=edge_index.dtype)
            src = jnp.concatenate([edge_index[0], loops])
            dst = jnp.concatenate([edge_index[1], loops])
            a_src = (h * att_src).sum(-1)
            a_dst = (h * att_dst).sum(-1)
            e = jax.nn.leaky_relu(a_src[src] + a_dst[dst], negative_slope=0.2)
            e_max = jax.ops.segment_max(e, dst, num_segments=M)
            ee = jnp.exp(e - e_max[dst])
            denom = jax.ops.segment_sum(ee, dst, num_segments=M)
            alpha = ee / (denom[dst] + 1e-16)
            msg = h[src] * alpha[:, :, None]
            agg = jax.ops.segment_sum(msg, dst, num_segments=M).reshape(M, HEADS * NUM_EXPERTS) + b_gat
            scores = _layernorm(agg, ln_gamma, ln_beta).reshape(M, HEADS, NUM_EXPERTS).mean(1)
            scores = scores.reshape(Bc, Nc, NUM_EXPERTS)
            topk_s, topk_i = jax.lax.top_k(scores, TOP_K)
            w = jax.nn.softmax(topk_s, axis=-1)
            out = jnp.zeros_like(x)
            for ei in range(NUM_EXPERTS):
                g = jnp.where(topk_i == ei, w, 0.0).sum(-1)
                hh = jax.nn.gelu(x @ W1[ei] + b1[ei], approximate=False)
                out = out + g[..., None] * (hh @ W2[ei] + b2[ei])
            return out
        key = jax.random.key(seed)
        ks = jax.random.split(key, 8)
        s = 0.05
        return {'x': jax.random.normal(ks[0], (B, N, D), jnp.float32), 'W_gat': jax.random.normal(ks[1], (D, HEADS * NUM_EXPERTS), jnp.float32) * s, 'att_src': jax.random.normal(ks[2], (HEADS, NUM_EXPERTS), jnp.float32) * s, 'att_dst': jax.random.normal(ks[3], (HEADS, NUM_EXPERTS), jnp.float32) * s, 'b_gat': jnp.zeros((HEADS * NUM_EXPERTS,), jnp.float32), 'ln_gamma': jnp.ones((HEADS * NUM_EXPERTS,), jnp.float32), 'ln_beta': jnp.zeros((HEADS * NUM_EXPERTS,), jnp.float32), 'W1': jax.random.normal(ks[4], (NUM_EXPERTS, D, 2 * D), jnp.float32) * s, 'b1': jnp.zeros((NUM_EXPERTS, 2 * D), jnp.float32), 'W2': jax.random.normal(ks[5], (NUM_EXPERTS, 2 * D, D), jnp.float32) * s, 'b2': jnp.zeros((NUM_EXPERTS, D), jnp.float32), 'edge_index': jax.random.randint(ks[6], (2, N_EDGES), 0, B * N, jnp.int32)}
    _L0_ffn_all = _L0_ffn_setup()
    _L0_ffn_in = {k: v for k, v in _L0_ffn_all.items() if k in ('W_gat', 'att_src', 'att_dst', 'b_gat', 'ln_gamma', 'ln_beta', 'W1', 'b1', 'W2', 'b2', 'edge_index', )}
    del _L0_ffn_all

    def _L1_attn_setup():
        import jax, jax.numpy as jnp
        import numpy as np
        NUM_HEADS = 8
        K_RATIO = 0.3
        LN_EPS = 1e-05

        def _layernorm(t, gamma, beta):
            mu = t.mean(axis=-1, keepdims=True)
            var = ((t - mu) ** 2).mean(axis=-1, keepdims=True)
            return (t - mu) * jax.lax.rsqrt(var + LN_EPS) * gamma + beta
        key = jax.random.key(seed)
        ks = jax.random.split(key, 5)
        B, N, C = (4096, 64, 256)
        hd = C // NUM_HEADS
        s = 0.02
        return {'x': jax.random.normal(ks[0], (B, N, C), jnp.float32), 'qkv_w': jax.random.normal(ks[1], (3 * C, C), jnp.float32) * s, 'qkv_b': jnp.zeros((3 * C,), jnp.float32), 'q_gamma': jnp.ones((hd,), jnp.float32), 'q_beta': jnp.zeros((hd,), jnp.float32), 'k_gamma': jnp.ones((hd,), jnp.float32), 'k_beta': jnp.zeros((hd,), jnp.float32), 'proj_w': jax.random.normal(ks[2], (C, C), jnp.float32) * s, 'proj_b': jnp.zeros((C,), jnp.float32)}
    _L1_attn_all = _L1_attn_setup()
    _L1_attn_in = {k: v for k, v in _L1_attn_all.items() if k in ('qkv_w', 'qkv_b', 'q_gamma', 'q_beta', 'k_gamma', 'k_beta', 'proj_w', 'proj_b', )}
    del _L1_attn_all

    def _L1_ffn_setup():
        import jax, jax.numpy as jnp
        import numpy as np
        B, T, D, H, E = (16, 4096, 256, 512, 8)
        key = jax.random.key(seed)
        ks = jax.random.split(key, 5)
        x = jax.random.normal(ks[0], (B, T, D), dtype=jnp.float32)
        gate_w = jax.random.normal(ks[1], (D, E), dtype=jnp.float32) * 0.02
        gate_b = jnp.zeros((E,), dtype=jnp.float32)
        W1 = jax.random.normal(ks[2], (E, D, H), dtype=jnp.float32) * 0.02
        b1 = jnp.zeros((E, H), dtype=jnp.float32)
        W2 = jax.random.normal(ks[3], (E, H, D), dtype=jnp.float32) * 0.02
        b2 = jnp.zeros((E, D), dtype=jnp.float32)
        return {'x': x, 'gate_w': gate_w, 'gate_b': gate_b, 'W1': W1, 'b1': b1, 'W2': W2, 'b2': b2}
    _L1_ffn_all = _L1_ffn_setup()
    _L1_ffn_in = {k: v for k, v in _L1_ffn_all.items() if k in ('gate_w', 'gate_b', 'W1', 'b1', 'W2', 'b2', )}
    del _L1_ffn_all

    return {
        "x": x,
        "L0_tok_A_log": _L0_tok_in["A_log"],
        "L0_tok_D": _L0_tok_in["D"],
        "L0_tok_W_dbc": _L0_tok_in["W_dbc"],
        "L0_tok_W_dt": _L0_tok_in["W_dt"],
        "L0_tok_b_dt": _L0_tok_in["b_dt"],
        "L0_attn_Lambda_re": _L0_attn_in["Lambda_re"],
        "L0_attn_Lambda_im": _L0_attn_in["Lambda_im"],
        "L0_attn_B": _L0_attn_in["B"],
        "L0_attn_C": _L0_attn_in["C"],
        "L0_attn_D": _L0_attn_in["D"],
        "L0_attn_log_step": _L0_attn_in["log_step"],
        "L0_ffn_W_gat": _L0_ffn_in["W_gat"],
        "L0_ffn_att_src": _L0_ffn_in["att_src"],
        "L0_ffn_att_dst": _L0_ffn_in["att_dst"],
        "L0_ffn_b_gat": _L0_ffn_in["b_gat"],
        "L0_ffn_ln_gamma": _L0_ffn_in["ln_gamma"],
        "L0_ffn_ln_beta": _L0_ffn_in["ln_beta"],
        "L0_ffn_W1": _L0_ffn_in["W1"],
        "L0_ffn_b1": _L0_ffn_in["b1"],
        "L0_ffn_W2": _L0_ffn_in["W2"],
        "L0_ffn_b2": _L0_ffn_in["b2"],
        "L0_ffn_edge_index": _L0_ffn_in["edge_index"],
        "L1_attn_qkv_w": _L1_attn_in["qkv_w"],
        "L1_attn_qkv_b": _L1_attn_in["qkv_b"],
        "L1_attn_q_gamma": _L1_attn_in["q_gamma"],
        "L1_attn_q_beta": _L1_attn_in["q_beta"],
        "L1_attn_k_gamma": _L1_attn_in["k_gamma"],
        "L1_attn_k_beta": _L1_attn_in["k_beta"],
        "L1_attn_proj_w": _L1_attn_in["proj_w"],
        "L1_attn_proj_b": _L1_attn_in["proj_b"],
        "L1_ffn_gate_w": _L1_ffn_in["gate_w"],
        "L1_ffn_gate_b": _L1_ffn_in["gate_b"],
        "L1_ffn_W1": _L1_ffn_in["W1"],
        "L1_ffn_b1": _L1_ffn_in["b1"],
        "L1_ffn_W2": _L1_ffn_in["W2"],
        "L1_ffn_b2": _L1_ffn_in["b2"],
    }

def reference(x, L0_tok_A_log, L0_tok_D, L0_tok_W_dbc, L0_tok_W_dt, L0_tok_b_dt, L0_attn_Lambda_re, L0_attn_Lambda_im, L0_attn_B, L0_attn_C, L0_attn_D, L0_attn_log_step, L0_ffn_W_gat, L0_ffn_att_src, L0_ffn_att_dst, L0_ffn_b_gat, L0_ffn_ln_gamma, L0_ffn_ln_beta, L0_ffn_W1, L0_ffn_b1, L0_ffn_W2, L0_ffn_b2, L0_ffn_edge_index, L1_attn_qkv_w, L1_attn_qkv_b, L1_attn_q_gamma, L1_attn_q_beta, L1_attn_k_gamma, L1_attn_k_beta, L1_attn_proj_w, L1_attn_proj_b, L1_ffn_gate_w, L1_ffn_gate_b, L1_ffn_W1, L1_ffn_b1, L1_ffn_W2, L1_ffn_b2):
    import jax
    import jax.numpy as jnp
    def _L0_tok_ref(x, A_log, D, W_dbc, W_dt, b_dt):
        import jax, jax.numpy as jnp
        import numpy as np
        BATCH = 2
        SEQ = 4096
        D_MODEL = 256
        N_STATE = 64
        DT_RANK = 1
        NUM_LAYERS = 3

        def _ssm_layer(x, A_log, Dp, W_dbc, W_dt, b_dt):
            A = -jnp.exp(A_log)
            dbc = jnp.einsum('ble,ce->blc', x, W_dbc)
            delta, Bm, Cm = jnp.split(dbc, [DT_RANK, DT_RANK + N_STATE], axis=-1)
            delta = jax.nn.softplus(jnp.einsum('blr,er->ble', delta, W_dt) + b_dt)
            dA = jnp.exp(delta[..., None] * A)
            dBx = (delta * x)[..., None] * Bm[:, :, None, :]

            def combine(c1, c2):
                a1, h1 = c1
                a2, h2 = c2
                return (a1 * a2, h1 * a2 + h2)
            _, hs = jax.lax.associative_scan(combine, (dA, dBx), axis=1)
            y = jnp.einsum('blen,bln->ble', hs, Cm)
            return y + Dp * x
        for i in range(NUM_LAYERS):
            x = _ssm_layer(x, A_log[i], D[i], W_dbc[i], W_dt[i], b_dt[i])
            if i < NUM_LAYERS - 1:
                b, l, d = x.shape
                x = x[:, :l // 2 * 2].reshape(b, l // 2, 2, d).mean(axis=2)
        return x

    def _L0_attn_ref(u, Lambda_re, Lambda_im, B, C, D, log_step):
        import jax, jax.numpy as jnp
        import numpy as np
        B_SZ, L, H, P = (16, 1024, 256, 256)
        DT_MIN, DT_MAX = (0.001, 0.1)

        def _binop(ei, ej):
            ai, bi = ei
            aj, bj = ej
            return (aj * ai, aj * bi + bj)
        Lambda = Lambda_re + 1j * Lambda_im
        B_tilde = B[..., 0] + 1j * B[..., 1]
        C_tilde = C[..., 0] + 1j * C[..., 1]
        Delta = jnp.exp(log_step[:, 0])
        Lambda_bar = jnp.exp(Lambda * Delta)
        B_bar = ((Lambda_bar - 1.0) / Lambda)[:, None] * B_tilde
        Bu = jnp.einsum('ph,blh->blp', B_bar, u.astype(B_bar.dtype))
        Lam = jnp.broadcast_to(Lambda_bar, Bu.shape)
        _, xs = jax.lax.associative_scan(_binop, (Lam, Bu), axis=1)
        ys = 2.0 * jnp.einsum('hp,blp->blh', C_tilde, xs).real
        return ys + D * u

    def _L0_ffn_ref(x, W_gat, att_src, att_dst, b_gat, ln_gamma, ln_beta, W1, b1, W2, b2, edge_index):
        import jax, jax.numpy as jnp
        import numpy as np
        B, N, D = (16, 4096, 256)
        NUM_EXPERTS, TOP_K, HEADS = (4, 2, 4)
        N_EDGES = 1048576
        LN_EPS = 1e-05

        def _layernorm(x, g, b):
            mu = x.mean(-1, keepdims=True)
            var = ((x - mu) ** 2).mean(-1, keepdims=True)
            return (x - mu) * jax.lax.rsqrt(var + LN_EPS) * g + b

        def _forward(x, edge_index, W_gat, att_src, att_dst, b_gat, ln_gamma, ln_beta, W1, b1, W2, b2):
            Bc, Nc, Dc = x.shape
            M = Bc * Nc
            x_flat = x.reshape(M, Dc)
            h = (x_flat @ W_gat).reshape(M, HEADS, NUM_EXPERTS)
            loops = jnp.arange(M, dtype=edge_index.dtype)
            src = jnp.concatenate([edge_index[0], loops])
            dst = jnp.concatenate([edge_index[1], loops])
            a_src = (h * att_src).sum(-1)
            a_dst = (h * att_dst).sum(-1)
            e = jax.nn.leaky_relu(a_src[src] + a_dst[dst], negative_slope=0.2)
            e_max = jax.ops.segment_max(e, dst, num_segments=M)
            ee = jnp.exp(e - e_max[dst])
            denom = jax.ops.segment_sum(ee, dst, num_segments=M)
            alpha = ee / (denom[dst] + 1e-16)
            msg = h[src] * alpha[:, :, None]
            agg = jax.ops.segment_sum(msg, dst, num_segments=M).reshape(M, HEADS * NUM_EXPERTS) + b_gat
            scores = _layernorm(agg, ln_gamma, ln_beta).reshape(M, HEADS, NUM_EXPERTS).mean(1)
            scores = scores.reshape(Bc, Nc, NUM_EXPERTS)
            topk_s, topk_i = jax.lax.top_k(scores, TOP_K)
            w = jax.nn.softmax(topk_s, axis=-1)
            out = jnp.zeros_like(x)
            for ei in range(NUM_EXPERTS):
                g = jnp.where(topk_i == ei, w, 0.0).sum(-1)
                hh = jax.nn.gelu(x @ W1[ei] + b1[ei], approximate=False)
                out = out + g[..., None] * (hh @ W2[ei] + b2[ei])
            return out
        return _forward(x, edge_index, W_gat, att_src, att_dst, b_gat, ln_gamma, ln_beta, W1, b1, W2, b2)

    def _L1_attn_ref(x, qkv_w, qkv_b, q_gamma, q_beta, k_gamma, k_beta, proj_w, proj_b):
        import jax, jax.numpy as jnp
        import numpy as np
        NUM_HEADS = 8
        K_RATIO = 0.3
        LN_EPS = 1e-05

        def _layernorm(t, gamma, beta):
            mu = t.mean(axis=-1, keepdims=True)
            var = ((t - mu) ** 2).mean(axis=-1, keepdims=True)
            return (t - mu) * jax.lax.rsqrt(var + LN_EPS) * gamma + beta
        B, N, C = x.shape
        H = NUM_HEADS
        hd = C // H
        scale = hd ** (-0.5)
        k_val = int(N * K_RATIO)
        qkv = (x @ qkv_w.T + qkv_b).reshape(B, N, 3, H, hd)
        qkv = jnp.transpose(qkv, (2, 0, 3, 1, 4))
        q, k, v = (qkv[0], qkv[1], qkv[2])
        q = _layernorm(q, q_gamma, q_beta)
        k = _layernorm(k, k_gamma, k_beta)
        attn = jnp.einsum('bhnd,bhmd->bhnm', q, k) * scale
        _, top_idx = jax.lax.top_k(attn, k_val)
        mask = jnp.full(attn.shape, -jnp.inf, attn.dtype)
        bi = jnp.arange(B)[:, None, None, None]
        hi = jnp.arange(H)[None, :, None, None]
        ni = jnp.arange(N)[None, None, :, None]
        mask = mask.at[bi, hi, ni, top_idx].set(0.0)
        attn = jax.nn.softmax(attn + mask, axis=-1)
        out = jnp.einsum('bhnm,bhmd->bhnd', attn, v)
        out = jnp.transpose(out, (0, 2, 1, 3)).reshape(B, N, C)
        return out @ proj_w.T + proj_b

    def _L1_ffn_ref(x, gate_w, gate_b, W1, b1, W2, b2):
        import jax, jax.numpy as jnp
        import numpy as np
        B, T, D, H, E = (16, 4096, 256, 512, 8)
        Bb, Tt, Dd = x.shape
        Ee = gate_w.shape[1]
        xf = x.reshape(-1, Dd)
        N = xf.shape[0]
        logits = xf @ gate_w + gate_b
        probs = jax.nn.softmax(logits, axis=-1)
        top2_vals, top2_idx = jax.lax.top_k(probs, 2)
        cw = jnp.zeros((N, Ee), dtype=xf.dtype).at[jnp.arange(N)[:, None], top2_idx].add(top2_vals)

        def step(acc, params):
            w1, bb1, w2, bb2, we = params
            h = jax.nn.gelu(xf @ w1 + bb1, approximate=False)
            y = h @ w2 + bb2
            return (acc + we[:, None] * y, None)
        out, _ = jax.lax.scan(step, jnp.zeros_like(xf), (W1, b1, W2, b2, cw.T))
        return out.reshape(Bb, Tt, Dd)

    h = _L0_tok_ref(x, L0_tok_A_log, L0_tok_D, L0_tok_W_dbc, L0_tok_W_dt, L0_tok_b_dt)
    h = h + _L0_attn_ref(_layernorm(h, axis=-1), L0_attn_Lambda_re, L0_attn_Lambda_im, L0_attn_B, L0_attn_C, L0_attn_D, L0_attn_log_step)
    h = h + _L0_ffn_ref(_layernorm(h, axis=-1), L0_ffn_W_gat, L0_ffn_att_src, L0_ffn_att_dst, L0_ffn_b_gat, L0_ffn_ln_gamma, L0_ffn_ln_beta, L0_ffn_W1, L0_ffn_b1, L0_ffn_W2, L0_ffn_b2, L0_ffn_edge_index)
    h = h + _L1_attn_ref(_layernorm(h, axis=-1), L1_attn_qkv_w, L1_attn_qkv_b, L1_attn_q_gamma, L1_attn_q_beta, L1_attn_k_gamma, L1_attn_k_beta, L1_attn_proj_w, L1_attn_proj_b)
    h = h + _L1_ffn_ref(_layernorm(h, axis=-1), L1_ffn_gate_w, L1_ffn_gate_b, L1_ffn_W1, L1_ffn_b1, L1_ffn_W2, L1_ffn_b2)
    return h


_drawn_inputs = setup_inputs


def setup_inputs(seed=0):
    import zlib

    import numpy as np

    out = dict(_drawn_inputs(seed))
    spreads = {'L0_tok_D': (1.0, 0.2),
     'L0_tok_b_dt': (0.0, 0.1),
     'L0_attn_Lambda_re': (-0.5, 0.6),
     'L0_ffn_b_gat': (0.0, 0.1),
     'L0_ffn_ln_gamma': (1.0, 0.2),
     'L0_ffn_ln_beta': (0.0, 0.365),
     'L0_ffn_b1': (0.0, 0.289),
     'L0_ffn_b2': (0.0, 0.1),
     'L1_attn_qkv_b': (0.0, 0.433),
     'L1_attn_q_gamma': (1.0, 0.6),
     'L1_attn_q_beta': (0.0, 0.8),
     'L1_attn_k_gamma': (1.0, 0.6),
     'L1_attn_k_beta': (0.0, 0.8),
     'L1_attn_proj_b': (0.0, 0.1),
     'L1_ffn_gate_b': (0.0, 0.8),
     'L1_ffn_b1': (0.0, 0.8),
     'L1_ffn_b2': (0.0, 0.604)}
    factors = {'L0_tok_W_dt': 3.715,
     'L0_ffn_att_src': 8.0,
     'L0_ffn_att_dst': 8.0,
     'L1_attn_qkv_w': 3.849,
     'L1_ffn_gate_w': 3.886,
     'L1_ffn_W1': 5.56,
     'L1_ffn_W2': 5.189}
    for name, (base, spread) in spreads.items():
        noise = np.random.default_rng([zlib.crc32(name.encode()), seed]).standard_normal(out[name].shape)
        drawn = base * np.exp(spread * noise) if base else spread * noise
        out[name] = jnp.asarray(drawn.astype(out[name].dtype))
    for name, factor in factors.items():
        out[name] = (out[name] * factor).astype(out[name].dtype)
    return out
```

```python
import concourse.bass as bass
from concourse import mybir
from contextlib import ExitStack

F32 = mybir.dt.float32
BF16 = mybir.dt.bfloat16
I32 = mybir.dt.int32
ALU = mybir.AluOpType
ACT = mybir.ActivationFunctionType
AX = mybir.AxisListType

P = 128
D = 256
KT = D // P
G = 512
NS = 64
NODES = 8192
NODE_BITS = 13
CODE_BITS = 2 * NODE_BITS + 1
TRASH = (NODES - 1) * NODES
EARLIER = 4096.0


class Phase:

    def __init__(self, nc, name):
        self.nc, self.name, self.ctx, self.used = nc, name, ExitStack(), []

    def __enter__(self):
        return self

    def __exit__(self, *a):
        self.ctx.close()
        self.nc.clear_and_free_semaphores(self.used)
        self.nc.all_engine_barrier()

    def sb(self, name, shape, dt=F32):
        return self.ctx.enter_context(self.nc.sbuf_tensor(f"{self.name}_{name}", shape, dt))

    def ps(self, name, shape, dt=F32):
        return self.ctx.enter_context(self.nc.psum_tensor(f"{self.name}_{name}", shape, dt))

    def sem(self, name):
        self.used.append(self.nc.alloc_semaphore(name=f"{self.name}_{name}"))
        return self.used[-1]

    def sems(self, name, n=2):
        return [self.sem(f"{name}{i}") for i in range(n)]

    def block(self):
        return self.ctx.enter_context(self.nc.Block())


def edge_phase(nc, edges_row, edges_col, codes, counts, key_cols, apart_total):
    C = 512
    n_chunks = edges_row.shape[2] // C
    with Phase(nc, "edge") as ph:
        zeros = ph.sb("zeros", [P, 8192])
        ones = ph.sb("ones", [P, 64])
        trash = ph.sb("trash", [P, 1], I32)
        raw = ph.sb("raw", [P, 2, 2, C], I32)
        key = ph.sb("key", [P, C], I32)
        dst = ph.sb("dst", [P, C], I32)
        bits = ph.sb("bits", [P, 2, C], I32)
        code = ph.sb("code", [P, 2, CODE_BITS, C], BF16)
        rawc = ph.sb("rawc", [P, 2, 2, C], I32)
        dropped = ph.sb("dropped", [P, C], I32)
        apart = ph.sb("apart", [P, C], I32)
        rows_in, cols_in, code_out = ph.sems("rows_in"), ph.sems("cols_in"), ph.sems("code_out")
        consts, rows_used, cols_used = ph.sem("consts"), ph.sem("rows_used"), ph.sem("cols_used")
        clear_a, clear_b, loops = ph.sem("clear_a"), ph.sem("clear_b"), ph.sem("loops")
        bit_ready, bit_used, step = ph.sem("bit_ready"), ph.sem("bit_used"), ph.sem("step")
        block = ph.block()
        table = NODES * NODES
        per = 8192 * P
        clears = [(counts[t], sem) for t, sem in ((0, clear_a), (1, clear_b))]

        @block.gpsimd
        def _(pool):
            nc.gpsimd.iota(trash[:], pattern=[[0, 1]], base=TRASH, channel_multiplier=1).then_inc(consts, 1)
            pool.wait_ge(consts, 3)
            for t, sem in clears:
                body = t[:, :].rearrange("(k p n) w -> p k (n w)", p=P, n=8192)
                for k in range(table // per):
                    pool.dma_start(body[:, k, :], zeros[:]).then_inc(sem, 16)
            pool.wait_ge(clear_a, 16 * (table // per))
            diagonal = t_diagonal(counts[0])
            with nc.allow_non_contiguous_dma(reason="one element per node, once"):
                pool.dma_start(diagonal, ones[:]).then_inc(loops, 16)
            pool.wait_ge(clear_b, 16 * (table // per))
            pool.wait_ge(loops, 16)

        @block.sync
        def _(sp):
            for c in range(n_chunks):
                u = c % 2
                if c >= 2:
                    sp.wait_ge(rows_used, c - 1)
                sp.dma_start(raw[:, u], edges_row[:, :, c * C:(c + 1) * C].rearrange("s p c -> p s c")).then_inc(rows_in[u], 16)
                if c >= 2:
                    sp.wait_ge(cols_used, c - 1)
                sp.dma_start(rawc[:, u], edges_col[:, :, c * C:(c + 1) * C].rearrange("s p c -> p s c")).then_inc(cols_in[u], 16)

        @block.vector
        def _(dve):
            nc.vector.memset(zeros[:], 0.0).then_inc(consts, 1)
            nc.vector.memset(apart_total[:], 0.0)
            nc.vector.memset(ones[:], 1.0).then_inc(consts, 1)
            n = 0
            for c in range(n_chunks):
                u = c % 2
                dve.wait_ge(rows_in[u], 16 * (c // 2 + 1))
                if c:
                    dve.wait_ge(bit_ready, CODE_BITS * c)
                nc.vector.tensor_scalar(key[:], raw[:, u, 0], float(NODES - 1), None, ALU.min).then_inc(step, 1)
                nc.vector.tensor_scalar(dst[:], raw[:, u, 1], float(NODES), None, ALU.min).then_inc(step, 1)
                dve.wait_ge(step, n + 2)
                nc.vector.tensor_scalar(key[:], key[:], NODE_BITS + 1, None, ALU.logical_shift_left).then_inc(step, 1)
                dve.wait_ge(step, n + 3)
                nc.vector.tensor_tensor(key[:], key[:], dst[:], ALU.bitwise_or).then_inc(rows_used, 1)
                dve.wait_ge(rows_used, c + 1)
                for b in range(CODE_BITS):
                    m = c * CODE_BITS + b
                    if m >= 2:
                        dve.wait_ge(bit_used, m - 1)
                    nc.vector.tensor_scalar(bits[:, m % 2], key[:], b, 1, ALU.logical_shift_right, ALU.bitwise_and).then_inc(bit_ready, 1)
                dve.wait_ge(cols_in[u], 16 * (c // 2 + 1))
                kc = key_cols[:, c * C:(c + 1) * C]
                nc.vector.tensor_scalar(kc, rawc[:, u, 0], float(NODES - 1), None, ALU.min).then_inc(step, 1)
                nc.vector.tensor_scalar(dropped[:], rawc[:, u, 1], float(NODES), None, ALU.is_ge).then_inc(step, 1)
                nc.vector.tensor_scalar(apart[:], rawc[:, u, 0], float(NODES - 1), None, ALU.is_ge).then_inc(step, 1)
                dve.wait_ge(step, n + 6)
                nc.vector.scalar_tensor_tensor(out=apart[:], in0=rawc[:, u, 1], scalar=float(P), in1=apart[:], op0=ALU.is_lt, op1=ALU.mult).then_inc(step, 1)
                dve.wait_ge(step, n + 7)
                nc.vector.tensor_tensor(dropped[:], dropped[:], apart[:], ALU.max).then_inc(step, 1)
                nc.vector.tensor_scalar(kc, kc, NODE_BITS, None, ALU.logical_shift_left).then_inc(step, 1)
                dve.wait_ge(step, n + 9)
                nc.vector.tensor_tensor(kc, kc, rawc[:, u, 1], ALU.bitwise_or).then_inc(cols_used, 1)
                dve.wait_ge(cols_used, c + 1)
                dve.wait_ge(consts, 3)
                nc.vector.copy_predicated(kc, dropped[:], trash[:].to_broadcast([P, C])).then_inc(step, 1)
                dve.wait_ge(step, n + 10)
                n += 10

        @block.scalar
        def _(act):
            for c in range(n_chunks):
                if c >= 2:
                    act.wait_ge(code_out[c % 2], 16 * CODE_BITS * (c // 2))
                for b in range(CODE_BITS):
                    m = c * CODE_BITS + b
                    act.wait_ge(bit_ready, m + 1)
                    nc.scalar.activation(code[:, c % 2, b], bits[:, m % 2], ACT.Copy, scale=2.0, bias=-1.0).then_inc(bit_used, 1)
                act.wait_ge(bit_used, CODE_BITS * (c + 1))
                for b in range(CODE_BITS):
                    act.dma_start(codes[b:b + 1, :].rearrange("o (p c) -> (o p) c", p=P)[:, c * C:(c + 1) * C], code[:, c % 2, b]).then_inc(code_out[c % 2], 16)
            for u in range(2):
                act.wait_ge(code_out[u], 16 * CODE_BITS * ((n_chunks + 1 - u) // 2))


def t_diagonal(table):
    return bass.AP(table.tensor, 0, [[(NODES + 1) * 64, P], [NODES + 1, 64]])


def project_phase(nc, name, tokens, xT, w_dbcT, w_dt, b_dt, layer, deltaT, uT, bc_parts):
    n_pairs = tokens // (2 * G)
    with Phase(nc, name) as ph:
        wT = ph.sb("wT", [P, KT, 1 + 2 * NS])
        w_delta = ph.sb("w_delta", [P, KT, P])
        w_bc = ph.sb("w_bc", [P, KT, 4, 96])
        dt_w = ph.sb("dt_w", [P, KT])
        dt_b = ph.sb("dt_b", [P, KT])
        x = ph.sb("x", [P, 2, KT, G])
        z = ph.sb("z", [P, 2, KT, G])
        soft = ph.sb("soft", [P, 2, KT, G])
        delta = ph.sb("delta", [P, 2, KT, G])
        u = ph.sb("u", [P, 2, KT, G])
        bc = ph.sb("bc", [96, 2, 4, G], BF16)
        rest = ph.sb("rest", [96, 2, 4, G])
        d_ps = ph.ps("d_ps", [P, 2, G])
        bc_ps = ph.ps("bc_ps", [P, 4, G])
        w_in, w_ready = ph.sem("w_in"), ph.sem("w_ready")
        x_in, stored = ph.sems("x_in"), ph.sems("stored")
        d_done, bc_done = ph.sem("d_done"), ph.sem("bc_done")
        z_done, bc_used = ph.sem("z_done"), ph.sem("bc_used")
        abs_done, ex_done, soft_done, step, u_done, cut = ph.sem("abs_done"), ph.sem("ex_done"), ph.sem("soft_done"), ph.sem("step"), ph.sem("u_done"), ph.sem("cut")
        block = ph.block()
        xv = xT.rearrange("(k p) (g t) -> p k g t", p=P, t=G)
        dv = deltaT.rearrange("(k p) (g t) -> p k g t", p=P, t=G)
        uv = uT.rearrange("(k p) (g t) -> p k g t", p=P, t=G)
        bcv = bc_parts.rearrange("p (g h t) -> p g h t", h=4, t=G)

        @block.sync
        def _(sp):
            sp.dma_start(wT[:], w_dbcT[layer].rearrange("(k p) c -> p k c", p=P)).then_inc(w_in, 16)
            with nc.allow_non_contiguous_dma(reason="two small vectors, once"):
                sp.dma_start(dt_w[:], w_dt[layer:layer + 1, :].rearrange("o (k p) -> (o p) k", p=P)).then_inc(w_in, 16)
                sp.dma_start(dt_b[:], b_dt[layer:layer + 1, :].rearrange("o (k p) -> (o p) k", p=P)).then_inc(w_in, 16)
            for q in range(2):
                sp.dma_start(x[:, q], xv[:, :, q]).then_inc(x_in[q], 16)
            with sp.Fori(1, n_pairs) as p:
                for q in range(2):
                    g = sp.snap(2 * p + q)
                    sp.wait_ge(u_done, 2 * p + q - 1)
                    sp.dma_start(x[:, q], xv[:, :, g]).then_inc(x_in[q], 16)

        @block.tensor
        def _(pe):
            pe.wait_ge(w_ready, 2)

            def project(first, p, q):
                g = 2 * p + q
                pe.wait_ge(x_in[q], 16 * (p + 1))
                if not first:
                    pe.wait_ge(z_done, g - 1)
                for k in range(KT):
                    last = nc.tensor.matmul(d_ps[:, q], w_delta[:, k], x[:, q, k], start=(k == 0), stop=(k == KT - 1))
                last.then_inc(d_done, 1)
                if not (first and q == 0):
                    pe.wait_ge(bc_used, g)
                for h in range(4):
                    for k in range(KT):
                        last = nc.tensor.matmul(bc_ps[0:96, h], w_bc[:, k, h], x[:, q, k], start=(k == 0), stop=(k == KT - 1))
                last.then_inc(bc_done, 1)

            for q in range(2):
                project(True, 0, q)
            with pe.Fori(1, n_pairs) as p:
                for q in range(2):
                    project(False, p, q)

        @block.scalar
        def _(act):
            def soften(first, p, q):
                g = 2 * p + q
                act.wait_ge(z_done, g + 1)
                nc.scalar.activation(soft[:, q], z[:, q], ACT.Abs).then_inc(abs_done, 1)
                act.wait_ge(abs_done, g + 1)
                nc.scalar.activation(soft[:, q], soft[:, q], ACT.Exp, scale=-1.0).then_inc(ex_done, 1)
                act.wait_ge(ex_done, g + 1)
                nc.scalar.activation(soft[:, q], soft[:, q], ACT.Ln, bias=1.0).then_inc(soft_done, 1)
                act.wait_ge(u_done, g + 1)
                act.wait_ge(cut, g + 1)
                act.dma_start(dv[:, :, g], delta[:, q]).then_inc(stored[q], 16)
                act.dma_start(uv[:, :, g], u[:, q]).then_inc(stored[q], 16)
                act.dma_start(bcv[:, g], bc[:, q]).then_inc(stored[q], 16)

            with act.Fori(0, n_pairs) as p:
                for q in range(2):
                    soften(False, p, q)
            for q in range(2):
                act.wait_ge(stored[q], 48 * n_pairs)

        @block.vector
        def _(dve):
            dve.wait_ge(w_in, 48)
            nc.vector.tensor_copy(w_delta[:], wT[:, :, 0:1].to_broadcast([P, KT, P])).then_inc(w_ready, 1)
            for h in range(4):
                for part in range(3):
                    last = nc.vector.tensor_copy(w_bc[:, :, h, 32 * part:32 * part + 32], wT[:, :, 1 + 32 * h:33 + 32 * h])
            last.then_inc(w_ready, 1)

            def finish(first, p, q):
                g = 2 * p + q
                if not first:
                    dve.wait_ge(stored[q], 48 * p)
                dve.wait_ge(d_done, g + 1)
                for k in range(KT):
                    last = nc.vector.tensor_scalar(z[:, q, k], d_ps[:, q], dt_w[:, k:k + 1], dt_b[:, k:k + 1], ALU.mult, ALU.add)
                last.then_inc(z_done, 1)
                dve.wait_ge(bc_done, g + 1)
                nc.vector.tensor_copy(bc[:, q], bc_ps[0:96]).then_inc(step, 1)
                dve.wait_ge(step, 4 * g + 1)
                nc.vector.tensor_tensor(rest[:, q], bc_ps[0:96], bc[:, q], ALU.subtract).then_inc(bc_used, 1)
                dve.wait_ge(bc_used, g + 1)
                nc.vector.tensor_copy(bc[32:64, q], rest[32:64, q])
                nc.vector.tensor_copy(bc[64:96, q], rest[64:96, q]).then_inc(step, 1)
                dve.wait_ge(soft_done, g + 1)
                nc.vector.scalar_tensor_tensor(out=delta[:, q], in0=z[:, q], scalar=0.0, in1=soft[:, q], op0=ALU.max, op1=ALU.add).then_inc(step, 1)
                dve.wait_ge(step, 4 * g + 2)
                nc.vector.tensor_tensor(rest[64:96, q], rest[64:96, q], bc[64:96, q], ALU.subtract).then_inc(step, 1)
                dve.wait_ge(step, 4 * g + 3)
                nc.vector.tensor_tensor(u[:, q], delta[:, q], x[:, q], ALU.mult).then_inc(u_done, 1)
                dve.wait_ge(step, 4 * g + 4)
                nc.vector.tensor_copy(bc[64:96, q], rest[64:96, q]).then_inc(cut, 1)

            for q in range(2):
                finish(True, 0, q)
            with dve.Fori(1, n_pairs) as p:
                for q in range(2):
                    finish(False, p, q)


def scan_phase(nc, name, tokens, seq, xT, deltaT, uT, bc_parts, A_log, Dp, layer, outT, pool_out,
               codes, counts, key_cols, apart_total, tile0, rounds):
    n_pairs = tokens // (2 * G)
    NI = NS // 4
    carry = seq > G
    seg = min(seq, G)
    OUT = G // 2 if pool_out else G
    n_tiles = G // P
    with Phase(nc, name) as ph:
        a_neg = ph.sb("a_neg", [P, KT, NS])
        d_col = ph.sb("d_col", [P, KT])
        sel = ph.sb("sel", [96, 32 * P], BF16)
        ident = ph.sb("ident", [P, P])
        order = ph.sb("order", [P, P])
        x = ph.sb("x", [P, 2, KT, G])
        delta = ph.sb("delta", [P, 2, KT, G])
        u = ph.sb("u", [P, 2, KT, G])
        bc = ph.sb("bc", [96, 2, 4, G], BF16)
        b_sb = ph.sb("b_sb", [P, 4, G])
        dA = ph.sb("dA", [P, 4, KT, G])
        dBx = ph.sb("dBx", [P, 4, KT, G])
        h = ph.sb("h", [P, 4, KT, G])
        hC = ph.sb("hC", [P, 4, KT, G])
        last_h = ph.sb("last_h", [P, KT, NS])
        y = ph.sb("y", [P, KT, G])
        out = ph.sb("out", [P, 2, KT, OUT])
        tile_codes = ph.sb("tile_codes", [CODE_BITS, n_tiles * P], BF16)
        equal = ph.sb("equal", [P, n_tiles, P], BF16)
        seen = ph.sb("seen", [P, n_tiles])
        is_first = ph.sb("is_first", [P, n_tiles], I32)
        keys = ph.sb("keys", [P, n_tiles], I32)
        rows = ph.sb("rows", [P, n_tiles], I32)
        spare = ph.sb("spare", [P, n_tiles], I32)
        bit = ph.sb("bit", [CODE_BITS, 1], I32)
        apart_bits = ph.sb("apart_bits", [CODE_BITS, P], I32)
        apart_codes = ph.sb("apart_codes", [CODE_BITS, P], BF16)
        hit = ph.sb("hit", [P, 4 * P], BF16)
        apart = ph.sb("apart", [P, 2 * n_pairs * NI * rounds])
        more = ph.sb("more", [P, 1])
        hit_bias = ph.sb("hit_bias", [P, 1])
        b_ps = ph.ps("b_ps", [P, 2, G])
        c_ps = ph.ps("c_ps", [P, 2, G])
        y_ps = ph.ps("y_ps", [P, KT, G])
        dots = ph.ps("dots", [P, G])
        hits = ph.ps("hits", [P, G])
        w_in, consts, a_exp, a_ready = ph.sem("w_in"), ph.sem("consts"), ph.sem("a_exp"), ph.sem("a_ready")
        hits_done, hits_used, apart_ready, apart_sum = ph.sem("hits_done"), ph.sem("hits_used"), ph.sem("apart_ready"), ph.sem("apart_sum")
        turn, first_sem, halved = ph.sem("turn"), ph.sem("first_sem"), ph.sem("halved")
        g_in = ph.sems("g_in")
        b_evac, bcast_b, bcast_c, dA_done = ph.sem("b_evac"), ph.sem("bcast_b"), ph.sem("bcast_c"), ph.sem("dA_done")
        dbx_pool, dbx_dve = ph.sem("dbx_pool"), ph.sem("dbx_dve")
        scan_done, hc_done, acc_done, y_evac, y_done = ph.sem("scan_done"), ph.sem("hc_done"), ph.sem("acc_done"), ph.sem("y_evac"), ph.sem("y_done")
        stored = ph.sems("stored")
        codes_in, dots_done, counted, chain, rows_ready = ph.sem("codes_in"), ph.sem("dots_done"), ph.sem("counted"), ph.sem("chain"), ph.sem("rows_ready")
        added = ph.sems("added")
        block = ph.block()
        xv = xT.rearrange("(k p) (g t) -> p k g t", p=P, t=G)
        dv = deltaT.rearrange("(k p) (g t) -> p k g t", p=P, t=G)
        uv = uT.rearrange("(k p) (g t) -> p k g t", p=P, t=G)
        bcv = bc_parts.rearrange("p (g h t) -> p g h t", h=4, t=G)
        ov = outT.rearrange("(k p) (g t) -> p k g t", p=P, t=OUT)
        cv = codes.rearrange("b (i e) -> b i e", e=P)

        def it_of(p, q, i):
            return (2 * p + q) * NI + i

        @block.sync
        def _(sp):
            sp.dma_start(a_neg[:], A_log[layer].rearrange("(k p) n -> p k n", p=P)).then_inc(w_in, 16)
            with nc.allow_non_contiguous_dma(reason="a small vector, once"):
                sp.dma_start(d_col[:], Dp[layer:layer + 1, :].rearrange("o (k p) -> (o p) k", p=P)).then_inc(w_in, 16)

            def load(q, g):
                sp.dma_start(x[:, q], xv[:, :, g]).then_inc(g_in[q], 16)
                sp.dma_start(delta[:, q], dv[:, :, g]).then_inc(g_in[q], 16)
                sp.dma_start(u[:, q], uv[:, :, g]).then_inc(g_in[q], 16)
                sp.dma_start(bc[:, q], bcv[:, g]).then_inc(g_in[q], 16)

            def load_codes(p, q, i):
                for r in range(rounds):
                    rd = it_of(p, q, i) * rounds + r
                    first = isinstance(rd, int) and rd == 0
                    t = rd * n_tiles + tile0
                    if not isinstance(rd, int):
                        t = sp.snap(t)
                    if not first:
                        sp.wait_ge(hits_done, rd)
                    sp.dma_start(tile_codes[:].rearrange("b (i e) -> b i e", e=P), cv[:, bass.ds(t, n_tiles), :]).then_inc(codes_in, 16)

            def group(p, q, first, last):
                load_codes(p, q, 0)
                load_codes(p, q, 1)
                if not first:
                    before = 2 * p + q - 1
                    after = 2 * p + q + 1
                    if not isinstance(p, int):
                        before, after = sp.snap(before), sp.snap(after)
                    sp.wait_ge(y_done, 2 * p + q)
                    sp.dma_start(ov[:, :, before], out[:, 1 - q]).then_inc(stored[1 - q], 16)
                    if not last:
                        load(1 - q, after)
                with sp.Fori(2, NI) as i:
                    load_codes(p, q, i)

            load(0, 0)
            load(1, 1)
            group(0, 0, True, False)
            group(0, 1, False, n_pairs == 1)
            if n_pairs > 2:
                with sp.Fori(1, n_pairs - 1) as p:
                    for q in range(2):
                        group(p, q, False, False)
            if n_pairs > 1:
                for q in range(2):
                    group(n_pairs - 1, q, False, q == 1)
            sp.wait_ge(y_done, 2 * n_pairs)
            sp.dma_start(ov[:, :, 2 * n_pairs - 1], out[:, 1]).then_inc(stored[1], 16)
            for q in range(2):
                sp.wait_ge(stored[q], 16 * n_pairs)

        @block.tensor
        def _(pe):
            pe.sem_inc(acc_done, 4)
            pe.wait_ge(consts, 12)
            pe.wait_ge(apart_ready, 2)

            def acc(p, q, i, j, start, stop):
                s = it_of(p, q, i) * 4 + j
                pe.wait_ge(hc_done, 2 + s + 1)
                if start:
                    pe.wait_ge(y_evac, 2 * p + q + 1)
                for k in range(KT):
                    last = nc.tensor.matmul(y_ps[:, k], ident[:], hC[:, j, k], start=start, stop=stop, skip_group_check=True)
                last.then_inc(acc_done, 1)

            def spread(p, q, i, j, what):
                half, off = j // 2, j % 2
                s = it_of(p, q, i) * 4 + j
                stationary = sel[:, bass.ds((2 * i + off) * P, P)]
                if what == "b":
                    pe.wait_ge(b_evac, s + 1)
                    nc.tensor.matmul(b_ps[:, j % 2], stationary, bc[:, q, half], start=True, stop=True).then_inc(bcast_b, 1)
                else:
                    pe.wait_ge(hc_done, s + 1)
                    nc.tensor.matmul(c_ps[:, j % 2], stationary, bc[:, q, 2 + half], start=True, stop=True).then_inc(bcast_c, 1)

            def compare(rd):
                pe.wait_ge(codes_in, 16 * (rd + 1))
                pe.wait_ge(counted, rd + 1)
                for t in range(n_tiles):
                    c = tile_codes[:, t * P:(t + 1) * P]
                    last = nc.tensor.matmul(dots[:, t * P:(t + 1) * P], c, c, start=True, stop=True)
                last.then_inc(dots_done, 1)
                pe.wait_ge(hits_used, rd + 1)
                nc.tensor.matmul(hits[:], apart_codes[:], tile_codes[:], start=True, stop=True).then_inc(hits_done, 1)

            def step(p, q, i, previous, following):
                it = it_of(p, q, i)
                spread(p, q, i, 2, "b")
                spread(p, q, i, 0, "c")
                spread(p, q, i, 3, "b")
                if previous:
                    acc(*previous[:3], 0, previous[3], False)
                    acc(*previous[:3], 1, False, False)
                    acc(*previous[:3], 2, False, False)
                spread(p, q, i, 1, "c")
                if previous:
                    acc(*previous[:3], 3, False, previous[4])
                if following:
                    if isinstance(following[2], int) and following[2] == 0:
                        pe.wait_ge(g_in[following[1]], 64 * (following[0] + 1))
                    spread(*following, 0, "b")
                    spread(*following, 1, "b")
                spread(p, q, i, 2, "c")
                for r in range(1, rounds + bool(following)):
                    compare(it * rounds + r)
                spread(p, q, i, 3, "c")

            def group(p, q, first, last):
                before = (p, 0) if q else (p - 1, 1)
                after = (p + 1, 0, 0) if q else (p, 1, 0)
                step(p, q, 0, None if first else (*before, NI - 1, False, True), (p, q, 1))
                step(p, q, 1, (p, q, 0, True, False), (p, q, 2))
                with pe.Fori(2, NI - 1) as i:
                    step(p, q, i, (p, q, i - 1, False, False), (p, q, i + 1))
                step(p, q, NI - 1, (p, q, NI - 2, False, False), None if last else after)

            pe.wait_ge(g_in[0], 64)
            spread(0, 0, 0, 0, "b")
            spread(0, 0, 0, 1, "b")
            compare(0)
            group(0, 0, True, False)
            group(0, 1, False, n_pairs == 1)
            if n_pairs > 2:
                with pe.Fori(1, n_pairs - 1) as p:
                    group(p, 0, False, False)
                    group(p, 1, False, False)
            if n_pairs > 1:
                group(n_pairs - 1, 0, False, False)
                group(n_pairs - 1, 1, False, True)
            for j in range(4):
                acc(n_pairs - 1, 1, NI - 1, j, False, j == 3)

        @block.scalar
        def _(act):
            act.wait_ge(w_in, 32)
            nc.scalar.activation(a_neg[:], a_neg[:], ACT.Exp).then_inc(a_exp, 1)
            act.wait_ge(a_ready, 1)
            act.wait_ge(consts, 12)
            act.sem_inc(b_evac, 2)

            act.sem_inc(hits_used, 1)

            def sum_hits(rd):
                act.wait_ge(hits_used, rd + 1)
                act.wait_ge(hits_done, rd + 1)
                nc.scalar.activation(hit[:], hits[:], ACT.Relu, bias=hit_bias[:, 0:1], accum_out=apart[:, bass.ds(rd, 1)]).then_inc(hits_used, 1)

            with act.Fori(0, n_pairs) as p:
                for q in range(2):
                    act.wait_ge(g_in[q], 64 * (p + 1))
                    with act.Fori(0, NI) as i:
                        it = it_of(p, q, i)
                        for j in range(4):
                            s = it * 4 + j
                            act.wait_ge(bcast_b, s + 1)
                            if j < 3:
                                act.wait_ge(dbx_pool, it * 3 + j + 1)
                            else:
                                act.wait_ge(dbx_dve, it + 1)
                            nc.scalar.activation(b_sb[:, j], b_ps[:, j % 2], ACT.Copy).then_inc(b_evac, 1)
                            act.wait_ge(scan_done, s + 1)
                            for k in range(KT):
                                n = 32 * (j // 2) + 2 * i + j % 2
                                last = nc.scalar.activation(dA[:, j, k], delta[:, q, k], ACT.Exp, scale=a_neg[:, k, bass.ds(n, 1)])
                            last.then_inc(dA_done, 1)
                        for r in range(rounds):
                            sum_hits(it * rounds + r)

        def dbx(eng, q, j):
            return eng.tensor_tensor(dBx[:, j], u[:, q], b_sb[:, j:j + 1].to_broadcast([P, KT, G]), ALU.mult)

        @block.gpsimd
        def _(pool):
            made = [0]

            def make(instruction):
                instruction.then_inc(consts, 1)
                made[0] += 1
                pool.wait_ge(consts, made[0])

            make(nc.gpsimd.memset(ident[:], 0.0))
            make(nc.gpsimd.memset(sel[:], 0.0))
            make(nc.gpsimd.memset(hit_bias[:], 1.0 - CODE_BITS))
            make(nc.gpsimd.memset(order[:], 1.0))
            make(nc.gpsimd.iota(spare[:], pattern=[[0, n_tiles]], base=TRASH, channel_multiplier=1))
            make(nc.gpsimd.iota(bit[:], pattern=[[0, 1]], base=0, channel_multiplier=1))
            make(nc.gpsimd.iota(apart_bits[:], pattern=[[1, P]], base=(NODES - 1) << (NODE_BITS + 1), channel_multiplier=0))
            make(nc.gpsimd.affine_select(out=ident[:], in_=ident[:], compare_op=ALU.not_equal, fill=1.0, base=0, pattern=[[-1, P]], channel_multiplier=1))
            for part in range(3):
                block32 = sel[32 * part:32 * part + 32].rearrange("k (n m) -> k n m", m=P)
                make(nc.gpsimd.affine_select(out=block32, in_=block32, compare_op=ALU.not_equal, fill=1.0, base=0, pattern=[[-1, 32], [0, P]], channel_multiplier=1))
            make(nc.gpsimd.affine_select(out=order[:], in_=order[:], compare_op=ALU.is_ge, fill=EARLIER, base=0, pattern=[[1, P]], channel_multiplier=-1))
            pool.sem_inc(dbx_pool, 3)

            def add(rd, t):
                table, k = t % 2, t // 2
                pool.wait_ge(added[table], 16 * (2 * rd + k))
                pool.sem_inc(turn, 1)
                pool.indirect_dma_start(out=counts[table], out_offset=bass.IndirectOffsetOnAxis(ap=rows[:, t:t + 1], axis=0),
                                        in_=seen[:, t:t + 1], in_offset=None, compute_op=ALU.add).then_inc(added[table], 16)

            with pool.Fori(0, n_pairs) as p:
                for q in range(2):
                    with pool.Fori(0, NI) as i:
                        it = it_of(p, q, i)
                        pool.wait_ge(g_in[q], 64 * (p + 1))
                        for j in range(3):
                            s = it * 4 + j
                            pool.wait_ge(b_evac, 2 + s + 1)
                            pool.wait_ge(scan_done, s + 1)
                            dbx(nc.gpsimd, q, j).then_inc(dbx_pool, 1)
                        for r in range(rounds):
                            pool.wait_ge(rows_ready, it * rounds + r + 1)
                            for t in range(n_tiles):
                                add(it * rounds + r, t)
            for table in range(2):
                pool.wait_ge(added[table], 16 * 2 * 2 * n_pairs * NI * rounds)

        @block.vector
        def _(dve):
            dve.wait_ge(a_exp, 1)
            nc.vector.tensor_scalar(a_neg[:], a_neg[:], -1.0, None, ALU.mult).then_inc(a_ready, 1)
            dve.sem_inc(hc_done, 2)
            dve.sem_inc(scan_done, 4)
            dve.sem_inc(dbx_dve, 1)
            dve.sem_inc(counted, 1)
            dve.sem_inc(y_evac, 1)
            dve.wait_ge(consts, 12)
            nc.vector.tensor_scalar(apart_bits[:], apart_bits[:], bit[:, 0:1], 1, ALU.logical_shift_right, ALU.bitwise_and).then_inc(apart_ready, 1)
            dve.wait_ge(apart_ready, 1)
            nc.vector.tensor_scalar(apart_codes[:], apart_bits[:], 2.0, -1.0, ALU.mult, ALU.add).then_inc(apart_ready, 1)

            def step(p, q, i):
                it = it_of(p, q, i)
                s0 = it * 4
                fresh = not (carry and q == 1)

                def scan(j):
                    n = 32 * (j // 2) + 2 * i + j % 2
                    dve.wait_ge(dA_done, s0 + j + 1)
                    if j < 3:
                        dve.wait_ge(dbx_pool, 3 + it * 3 + j + 1)
                    else:
                        dve.wait_ge(dbx_dve, it + 2)
                    for k in range(KT):
                        for c in range(0, G, seg):
                            initial = 0.0 if fresh else last_h[:, k, bass.ds(n, 1)]
                            last = nc.vector.tensor_tensor_scan(h[:, j, k, c:c + seg], dA[:, j, k, c:c + seg], dBx[:, j, k, c:c + seg], initial, ALU.mult, ALU.add)
                    last.then_inc(scan_done, 1)

                def times_c(j):
                    n = 32 * (j // 2) + 2 * i + j % 2
                    dve.wait_ge(scan_done, 4 + s0 + j + 1)
                    dve.wait_ge(bcast_c, s0 + j + 1)
                    dve.wait_ge(acc_done, s0 + j + 1)
                    if carry and q == 0:
                        nc.vector.tensor_copy(last_h[:, :, bass.ds(n, 1)], h[:, j, :, G - 1:G]).then_inc(chain, 1)
                    nc.vector.tensor_tensor(hC[:, j], h[:, j], c_ps[:, j % 2:j % 2 + 1].to_broadcast([P, KT, G]), ALU.mult).then_inc(hc_done, 1)

                def count(rd):
                    dve.wait_ge(dots_done, rd + 1)
                    for table in range(2):
                        dve.wait_ge(added[table], 32 * rd)
                    for t in range(n_tiles):
                        last = nc.vector.scalar_tensor_tensor(out=equal[:, t], in0=dots[:, t * P:(t + 1) * P], scalar=CODE_BITS - 0.5, in1=order[:],
                                                              op0=ALU.is_ge, op1=ALU.mult, accum_out=seen[:, t:t + 1])
                    last.then_inc(counted, 1)
                    nc.vector.tensor_copy(rows[:], spare[:])
                    nc.vector.tensor_copy(keys[:], key_cols[:, bass.ds(rd * n_tiles + tile0, n_tiles)])
                    dve.wait_ge(counted, rd + 2)
                    nc.vector.tensor_scalar(is_first[:], seen[:], EARLIER, None, ALU.is_lt).then_inc(first_sem, 1)

                def place():
                    nc.vector.copy_predicated(rows[:], is_first[:], keys[:]).then_inc(rows_ready, 1)

                scan(0)
                count(it * rounds)
                dve.wait_ge(b_evac, 2 + s0 + 4)
                dbx(nc.vector, q, 3).then_inc(dbx_dve, 1)
                scan(1)
                dve.wait_ge(first_sem, it * rounds + 1)
                times_c(0)
                place()
                times_c(1)
                scan(2)
                for r in range(1, rounds):
                    count(it * rounds + r)
                scan(3)
                for r in range(1, rounds):
                    dve.wait_ge(first_sem, it * rounds + r + 1)
                times_c(2)
                if rounds > 1:
                    place()
                times_c(3)

            def evacuate(p, q):
                g = 2 * p + q
                dve.wait_ge(acc_done, 4 + (g + 1) * NI * 4)
                if not (isinstance(p, int) and p == 0):
                    dve.wait_ge(stored[q], 16 * p)
                for k in range(KT):
                    last = nc.vector.scalar_tensor_tensor(out=y[:, k], in0=x[:, q, k], scalar=d_col[:, k:k + 1], in1=y_ps[:, k], op0=ALU.mult, op1=ALU.add)
                last.then_inc(y_evac, 1)
                dve.wait_ge(y_evac, 1 + g + 1)
                if pool_out:
                    pairs = y[:].rearrange("p k (t two) -> p k t two", two=2)
                    nc.vector.tensor_tensor(out[:, q], pairs[:, :, :, 0], pairs[:, :, :, 1], ALU.add).then_inc(halved, 1)
                    dve.wait_ge(halved, g + 1)
                    nc.vector.tensor_scalar(out[:, q], out[:, q], 0.5, None, ALU.mult).then_inc(y_done, 1)
                else:
                    nc.vector.tensor_copy(out[:, q], y[:]).then_inc(y_done, 1)

            def group(p, q, first):
                dve.wait_ge(g_in[q], 64 * (p + 1))
                if carry and q == 1:
                    dve.wait_ge(chain, NS * (p + 1))
                step(p, q, 0)
                if not first:
                    evacuate(*((p, 0) if q else (p - 1, 1)))
                with dve.Fori(1, NI) as i:
                    step(p, q, i)

            group(0, 0, True)
            group(0, 1, False)
            if n_pairs > 1:
                with dve.Fori(1, n_pairs) as p:
                    group(p, 0, False)
                    group(p, 1, False)
            evacuate(n_pairs - 1, 1)
            dve.wait_ge(hits_used, 1 + 2 * n_pairs * NI * rounds)
            nc.vector.tensor_reduce(more[:], apart[:], AX.X, ALU.add).then_inc(apart_sum, 1)
            dve.wait_ge(apart_sum, 1)
            nc.vector.tensor_tensor(apart_total[:], apart_total[:], more[:], ALU.add).then_inc(apart_sum, 1)
            dve.wait_ge(apart_sum, 2)
EPS = 1e-5
TWO_PI = 6.283185307179586
BIG = 3.0e38


class Chain:

    def __init__(self, eng, sem):
        self.eng, self.sem, self.n = eng, sem, 0

    def __call__(self, instruction):
        instruction.then_inc(self.sem, 1)
        self.n += 1
        self.eng.wait_ge(self.sem, self.n)


def identity(nc, pool, ident, made, n=1):
    nc.gpsimd.memset(ident[:], 0.0).then_inc(made, 1)
    pool.wait_ge(made, 1)
    nc.gpsimd.affine_select(out=ident[:], in_=ident[:], compare_op=ALU.not_equal, fill=1.0, base=0,
                            pattern=[[-1, P]], channel_multiplier=1).then_inc(made, 1)


def mix_phase(nc, hT, lam_re, lam_im, log_step, b_t, c_t, d_vec, w_gat, att_src, h1, zT, gat_h, gat_src):
    SEQ = 256
    NG = NODES // G
    T4 = G // P
    with Phase(nc, "mix") as ph:
        lre, lim, stp = ph.sb("lre", [P, KT]), ph.sb("lim", [P, KT]), ph.sb("stp", [P, KT])
        small = ph.sb("small", [P, 24, KT])
        cosT, sinT = ph.sb("cosT", [P, KT, SEQ]), ph.sb("sinT", [P, KT, SEQ])
        g_re, g_im = ph.sb("g_re", [P, KT, SEQ]), ph.sb("g_im", [P, KT, SEQ])
        rad = ph.sb("rad", [P, KT, SEQ])
        tmp = ph.sb("tmp", [P, SEQ])
        bw = ph.sb("bw", [P, 2, KT, D])
        cw = ph.sb("cw", [P, 2, KT, D])
        d_row = ph.sb("d_row", [P, D])
        wg = ph.sb("wg", [P, KT, 16])
        asrc_row = ph.sb("asrc_row", [P, 16])
        ident = ph.sb("ident", [P, P])
        h_in = ph.sb("h_in", [P, 2, KT, G])
        h = ph.sb("h", [P, T4, D])
        u = ph.sb("u", [P, T4, D])
        uT = ph.sb("uT", [P, KT, G])
        v = ph.sb("v", [P, 2, KT, G])
        v2 = ph.sb("v2", [P, 2, KT, G])
        s = ph.sb("s", [P, 2, KT, G])
        xs = ph.sb("xs", [P, 2, KT, G])
        stats, mv, dev = ph.sb("stats", [P, T4, 6]), ph.sb("mv", [P, T4, 2]), ph.sb("dev", [P, T4, 3])
        h1_sb = ph.sb("h1_sb", [P, T4, D])
        z = ph.sb("z", [P, T4, D])
        zT_sb = ph.sb("zT_sb", [P, KT, G])
        ghs = ph.sb("ghs", [P, T4, 16])
        tr = ph.ps("tr", [P, 4 * G // 2])
        bu = ph.ps("bu", [P, 2, KT, G])
        y = ph.ps("y", [P, T4, D])
        S = {n: ph.sem(n) for n in (
            "w_in made chain h_tr h_tok stat1 std1 u_ready u_tr uT_ready bu_done v_ready xs_ready y_done "
            "h1_ready stat2 std2 z_ready z_tr zT_ready gat_done gat_saved stored_h stored_z sub cwneg turn").split()}
        hin = ph.sems("hin")
        block = ph.block()
        hv = hT.rearrange("(k p) (g t) -> p k g t", p=P, t=G)
        zv = zT.rearrange("(k p) (g t) -> p k g t", p=P, t=G)
        h1v = h1.rearrange("(g t p) d -> p g t d", p=P, t=T4)
        trt = tr[:].rearrange("p (t d) -> p t d", d=D)
        trw = tr[:].rearrange("p (k t) -> p k t", t=G)
        N_W = 10

        @block.sync
        def _(sp):
            with nc.allow_non_contiguous_dma(reason="small vectors, once"):
                for t, a in ((lre, lam_re), (lim, lam_im), (stp, log_step)):
                    sp.dma_start(t[:], a.rearrange("(k p) -> p k", p=P)).then_inc(S["w_in"], 16)
            for ri in range(2):
                sp.dma_start(bw[:, ri], b_t[ri].rearrange("(k p) n -> p k n", p=P)).then_inc(S["w_in"], 16)
                sp.dma_start(cw[:, ri], c_t[ri].rearrange("(k p) n -> p k n", p=P)).then_inc(S["w_in"], 16)
            sp.dma_start(d_row[:], d_vec.partition_broadcast(P)).then_inc(S["w_in"], 16)
            sp.dma_start(asrc_row[:], att_src.partition_broadcast(P)).then_inc(S["w_in"], 16)
            sp.dma_start(wg[:], w_gat.rearrange("(k p) n -> p k n", p=P)).then_inc(S["w_in"], 16)
            for q in range(2):
                sp.dma_start(h_in[:, q], hv[:, :, q]).then_inc(hin[q], 16)
            with sp.Fori(1, NG // 2) as p:
                for q in range(2):
                    g = sp.snap(2 * p + q)
                    sp.wait_ge(S["h_tr"], 2 * p + q - 1)
                    sp.dma_start(h_in[:, q], hv[:, :, g]).then_inc(hin[q], 16)

        @block.gpsimd
        def _(pool):
            identity(nc, pool, ident, S["made"])

        @block.tensor
        def _(pe):
            pe.wait_ge(S["made"], 2)
            pe.wait_ge(S["w_in"], 16 * N_W)
            pe.wait_ge(S["cwneg"], 1)
            with pe.Fori(0, NG // 2) as p:
                for q in range(2):
                    g = 2 * p + q
                    pe.wait_ge(hin[q], 16 * (p + 1))
                    pe.wait_ge(S["zT_ready"], g)
                    for t in range(T4):
                        for k in range(KT):
                            last = nc.tensor.transpose(trt[:, t, k * P:(k + 1) * P], h_in[:, q, k, t * P:(t + 1) * P], ident[:])
                    last.then_inc(S["h_tr"], 1)
                    pe.wait_ge(S["h_tok"], g + 1)
                    pe.wait_ge(S["u_ready"], g + 1)
                    for t in range(T4):
                        for k in range(KT):
                            last = nc.tensor.transpose(trw[:, k, t * P:(t + 1) * P], u[:, t, k * P:(k + 1) * P], ident[:])
                    last.then_inc(S["u_tr"], 1)
                    pe.wait_ge(S["uT_ready"], g + 1)
                    for ri in range(2):
                        for m in range(KT):
                            for k in range(KT):
                                last = nc.tensor.matmul(bu[:, ri, m], bw[:, ri, k, m * P:(m + 1) * P], uT[:, k], start=(k == 0), stop=(k == KT - 1))
                    last.then_inc(S["bu_done"], 1)
                    pe.wait_ge(S["xs_ready"], g + 1)
                    pe.wait_ge(S["gat_saved"], g)
                    for t in range(T4):
                        for ri in range(2):
                            for k in range(KT):
                                last = nc.tensor.matmul(y[:, t], xs[:, ri, k, t * P:(t + 1) * P], cw[:, ri, k], start=(ri + k == 0), stop=(ri + k == 2))
                    last.then_inc(S["y_done"], 1)
                    pe.wait_ge(S["z_ready"], g + 1)
                    for t in range(T4):
                        for k in range(KT):
                            last = nc.tensor.transpose(trw[:, k, t * P:(t + 1) * P], z[:, t, k * P:(k + 1) * P], ident[:])
                    last.then_inc(S["z_tr"], 1)
                    pe.wait_ge(S["zT_ready"], g + 1)
                    for t in range(T4):
                        for k in range(KT):
                            last = nc.tensor.matmul(y[:, t, 0:16], zT_sb[:, k, t * P:(t + 1) * P], wg[:, k], start=(k == 0), stop=(k == KT - 1))
                    last.then_inc(S["gat_done"], 1)

        @block.scalar
        def _(act):
            act.wait_ge(S["w_in"], 16 * N_W)
            nc.scalar.activation(small[:, 0], stp[:], ACT.Exp).then_inc(S["sub"], 1)
            act.wait_ge(S["sub"], 2)
            nc.scalar.activation(small[:, 3], small[:, 1], ACT.Exp).then_inc(S["sub"], 1)
            nc.scalar.activation(small[:, 4], small[:, 7], ACT.Sin).then_inc(S["sub"], 1)
            nc.scalar.activation(small[:, 5], small[:, 8], ACT.Sin).then_inc(S["sub"], 1)
            with act.Fori(0, NG) as g:
                act.wait_ge(S["h_tr"], g + 1)
                act.wait_ge(S["h1_ready"], g)
                nc.scalar.activation(h[:], trt, ACT.Copy).then_inc(S["h_tok"], 1)
                act.wait_ge(S["stat1"], g + 1)
                nc.scalar.activation(dev[:, :, 1], dev[:, :, 0], ACT.Sqrt).then_inc(S["std1"], 1)
                act.wait_ge(S["u_tr"], g + 1)
                nc.scalar.activation(uT[:], trw, ACT.Copy).then_inc(S["uT_ready"], 1)
                act.wait_ge(S["stat2"], g + 1)
                nc.scalar.activation(dev[:, :, 1], dev[:, :, 0], ACT.Sqrt).then_inc(S["std2"], 1)
                act.wait_ge(S["h1_ready"], g + 1)
                act.dma_start(h1v[:, g], h1_sb[:]).then_inc(S["stored_h"], 16)
                act.wait_ge(S["z_tr"], g + 1)
                act.wait_ge(S["stored_z"], 16 * g)
                nc.scalar.activation(zT_sb[:], trw, ACT.Copy).then_inc(S["zT_ready"], 1)
                act.wait_ge(S["zT_ready"], g + 1)
                act.dma_start(zv[:, :, g], zT_sb[:]).then_inc(S["stored_z"], 16)
            act.wait_ge(S["stored_h"], 16 * NG)
            act.wait_ge(S["stored_z"], 16 * NG)

        @block.vector
        def _(dve):
            V = nc.vector
            link = Chain(dve, S["chain"])
            q_ = lambda n: small[:, n]
            dve.wait_ge(S["w_in"], 16 * N_W)
            V.tensor_scalar(cw[:, 0], cw[:, 0], 2.0, None, ALU.mult)
            V.tensor_scalar(cw[:, 1], cw[:, 1], -2.0, None, ALU.mult).then_inc(S["cwneg"], 1)
            dve.wait_ge(S["sub"], 1)
            link(V.tensor_tensor(q_(2), lim[:], q_(0), ALU.mult))
            link(V.tensor_scalar(q_(6), q_(2), 1.0 / TWO_PI, None, ALU.mult))
            link(V.tensor_scalar(q_(6), q_(6), 12582912.0, None, ALU.add))
            link(V.tensor_scalar(q_(6), q_(6), 12582912.0, None, ALU.subtract))
            c1 = 6.28125
            c2 = 0.0019350051879882812
            c3 = TWO_PI - c1 - c2
            link(V.scalar_tensor_tensor(out=q_(7), in0=q_(6), scalar=-c1, in1=q_(2), op0=ALU.mult, op1=ALU.add))
            link(V.scalar_tensor_tensor(out=q_(7), in0=q_(6), scalar=-c2, in1=q_(7), op0=ALU.mult, op1=ALU.add))
            link(V.scalar_tensor_tensor(out=q_(7), in0=q_(6), scalar=-c3, in1=q_(7), op0=ALU.mult, op1=ALU.add))
            link(V.tensor_scalar(q_(8), q_(7), TWO_PI / 4, None, ALU.add))
            link(V.tensor_scalar(q_(9), q_(8), TWO_PI / 2, -TWO_PI, ALU.is_gt, ALU.mult))
            link(V.tensor_tensor(q_(8), q_(8), q_(9), ALU.add))
            link(V.tensor_scalar(q_(8), q_(8), 3.141592, -3.141592, ALU.min, ALU.max))
            link(V.tensor_scalar(q_(7), q_(7), 3.141592, -3.141592, ALU.min, ALU.max))
            V.tensor_tensor(q_(1), lre[:], q_(0), ALU.mult).then_inc(S["sub"], 1)
            dve.wait_ge(S["sub"], 5)
            link(V.tensor_tensor(q_(10), q_(3), q_(5), ALU.mult))
            link(V.tensor_scalar(q_(10), q_(10), -1.0, None, ALU.add))
            link(V.tensor_tensor(q_(11), q_(3), q_(4), ALU.mult))
            link(V.tensor_tensor(q_(12), lre[:], lre[:], ALU.mult))
            link(V.tensor_tensor(q_(13), lim[:], lim[:], ALU.mult))
            link(V.tensor_tensor(q_(12), q_(12), q_(13), ALU.add))
            link(V.reciprocal(q_(12), q_(12)))
            link(V.tensor_tensor(q_(13), q_(10), lre[:], ALU.mult))
            link(V.tensor_tensor(q_(14), q_(11), lim[:], ALU.mult))
            link(V.tensor_tensor(q_(13), q_(13), q_(14), ALU.add))
            link(V.tensor_tensor(q_(13), q_(13), q_(12), ALU.mult))
            link(V.tensor_tensor(q_(14), q_(11), lre[:], ALU.mult))
            link(V.tensor_tensor(q_(15), q_(10), lim[:], ALU.mult))
            link(V.tensor_tensor(q_(14), q_(14), q_(15), ALU.subtract))
            link(V.tensor_tensor(q_(14), q_(14), q_(12), ALU.mult))
            link(V.memset(cosT[:, :, 0:1], 1.0))
            link(V.memset(sinT[:, :, 0:1], 0.0))
            link(V.tensor_copy(q_(16), q_(5)))
            link(V.tensor_copy(q_(17), q_(4)))
            n = 1
            while n < SEQ:
                for k in range(KT):
                    wc, ws = small[:, 16, k:k + 1], small[:, 17, k:k + 1]
                    link(V.tensor_scalar(tmp[:, 0:n], sinT[:, k, 0:n], ws, None, ALU.mult))
                    link(V.scalar_tensor_tensor(out=cosT[:, k, n:2 * n], in0=cosT[:, k, 0:n], scalar=wc, in1=tmp[:, 0:n], op0=ALU.mult, op1=ALU.subtract))
                    link(V.tensor_scalar(tmp[:, 0:n], sinT[:, k, 0:n], wc, None, ALU.mult))
                    link(V.scalar_tensor_tensor(out=sinT[:, k, n:2 * n], in0=cosT[:, k, 0:n], scalar=ws, in1=tmp[:, 0:n], op0=ALU.mult, op1=ALU.add))
                link(V.tensor_tensor(q_(18), q_(17), q_(17), ALU.mult))
                link(V.tensor_tensor(q_(19), q_(16), q_(17), ALU.mult))
                link(V.tensor_tensor(q_(16), q_(16), q_(16), ALU.mult))
                link(V.tensor_tensor(q_(16), q_(16), q_(18), ALU.subtract))
                link(V.tensor_scalar(q_(17), q_(19), 2.0, None, ALU.mult))
                n *= 2
            for k in range(KT):
                fr, fi = small[:, 13, k:k + 1], small[:, 14, k:k + 1]
                link(V.tensor_scalar(tmp[:], sinT[:, k], fi, None, ALU.mult))
                link(V.scalar_tensor_tensor(out=g_re[:, k], in0=cosT[:, k], scalar=fr, in1=tmp[:], op0=ALU.mult, op1=ALU.add))
                link(V.tensor_scalar(tmp[:], sinT[:, k], fr, None, ALU.mult))
                link(V.scalar_tensor_tensor(out=g_im[:, k], in0=cosT[:, k], scalar=fi, in1=tmp[:], op0=ALU.mult, op1=ALU.subtract))
                link(V.tensor_copy(rad[:, k], small[:, 3, k:k + 1].to_broadcast([P, SEQ])))
            base = link.n

            def seqs(a):
                return a.rearrange("p k (b t) -> p k b t", t=SEQ)

            def norm(x, out, stat, std, ready, g, c):
                def ch(i):
                    i.then_inc(S["chain"], 1)
                    c[0] += 1
                    dve.wait_ge(S["chain"], base + g * PER + c[0])
                for t in range(T4):
                    last = V.bn_stats(stats[:, t], x[:, t])
                ch(last)
                dve.sem_inc(S["turn"], 1)
                for t in range(T4):
                    last = V.bn_aggr(mv[:, t], stats[:, t])
                ch(last)
                V.tensor_scalar(dev[:, :, 0], mv[:, :, 1], EPS, None, ALU.add).then_inc(S[stat], 1)
                dve.wait_ge(S[std], g + 1)
                ch(V.reciprocal(dev[:, :, 2], dev[:, :, 1]))
                for t in range(T4):
                    last = V.tensor_scalar(out[:, t], x[:, t], mv[:, t, 0:1], dev[:, t, 2:3], ALU.subtract, ALU.mult)
                last.then_inc(S[ready], 1)

            PER = 16

            with dve.Fori(0, NG) as g:
                c = [0]

                def ch(i):
                    i.then_inc(S["chain"], 1)
                    c[0] += 1
                    dve.wait_ge(S["chain"], base + g * PER + c[0])

                dve.wait_ge(S["h_tok"], g + 1)
                norm(h, u, "stat1", "std1", "u_ready", g, c)
                dve.wait_ge(S["bu_done"], g + 1)
                for i, (a0, t0, a1, t1, op) in enumerate(((0, g_re, 1, g_im, ALU.subtract), (0, g_im, 1, g_re, ALU.add))):
                    for k in range(KT):
                        V.tensor_tensor(v[:, i, k].rearrange("p (b t) -> p b t", t=SEQ), bu[:, a0, k].rearrange("p (b t) -> p b t", t=SEQ),
                                        t0[:, k:k + 1].to_broadcast([P, 2, SEQ]), ALU.mult)
                        last = V.tensor_tensor(v2[:, i, k].rearrange("p (b t) -> p b t", t=SEQ), bu[:, a1, k].rearrange("p (b t) -> p b t", t=SEQ),
                                               t1[:, k:k + 1].to_broadcast([P, 2, SEQ]), ALU.mult)
                ch(last)
                V.tensor_tensor(v[:, 0], v[:, 0], v2[:, 0], ALU.subtract)
                ch(V.tensor_tensor(v[:, 1], v[:, 1], v2[:, 1], ALU.add))
                for i in range(2):
                    for k in range(KT):
                        for b in range(2):
                            last = V.tensor_tensor_scan(s[:, i, k, b * SEQ:(b + 1) * SEQ], rad[:, k], v[:, i, k, b * SEQ:(b + 1) * SEQ], 0.0, ALU.mult, ALU.add)
                ch(last)
                for i, (t0, t1) in enumerate(((cosT, sinT), (sinT, cosT))):
                    for k in range(KT):
                        V.tensor_tensor(v[:, i, k].rearrange("p (b t) -> p b t", t=SEQ), s[:, 0, k].rearrange("p (b t) -> p b t", t=SEQ),
                                        t0[:, k:k + 1].to_broadcast([P, 2, SEQ]), ALU.mult)
                        last = V.tensor_tensor(v2[:, i, k].rearrange("p (b t) -> p b t", t=SEQ), s[:, 1, k].rearrange("p (b t) -> p b t", t=SEQ),
                                               t1[:, k:k + 1].to_broadcast([P, 2, SEQ]), ALU.mult)
                ch(last)
                V.tensor_tensor(xs[:, 0], v[:, 0], v2[:, 0], ALU.subtract)
                V.tensor_tensor(xs[:, 1], v[:, 1], v2[:, 1], ALU.add).then_inc(S["xs_ready"], 1)
                dve.wait_ge(S["stored_h"], 16 * g)
                V.tensor_tensor(z[:], u[:], d_row[:].rearrange("p (o d) -> p o d", o=1).to_broadcast([P, T4, D]), ALU.mult)
                ch(V.tensor_copy(stats[:, 0, 0:1], mv[:, 0, 0:1]))
                ch(V.tensor_tensor(z[:], z[:], h[:], ALU.add))
                dve.wait_ge(S["y_done"], g + 1)
                V.tensor_tensor(h1_sb[:], z[:], y[:], ALU.add).then_inc(S["h1_ready"], 1)
                dve.wait_ge(S["h1_ready"], g + 1)
                norm(h1_sb, z, "stat2", "std2", "z_ready", g, c)
                dve.wait_ge(S["gat_done"], g + 1)
                ch(V.tensor_copy(gat_h[:, bass.ds(g * T4, T4), :], y[:, :, 0:16]))
                ch(V.tensor_tensor(ghs[:], y[:, :, 0:16], asrc_row[:].rearrange("p (o d) -> p o d", o=1).to_broadcast([P, T4, 16]), ALU.mult))
                V.tensor_reduce(gat_src[:, bass.ds(g * T4, T4), :], ghs[:].rearrange("p t (h e) -> p t h e", e=4), AX.X, ALU.add).then_inc(S["gat_saved"], 1)
                assert c[0] <= PER
                while c[0] < PER:
                    ch(V.tensor_copy(stats[:, 0, 1:2], mv[:, 0, 0:1]))


def bcast(row, shape):
    return row.rearrange("p (o d) -> p o d", o=1).to_broadcast(shape)


def best_two(V, link, s, first, second, pick, top, rank_row, E):
    n = s.shape[1]
    for i, hot in enumerate((first, second)):
        link(V.tensor_reduce(top[:, :, i:i + 1], s, AX.X, ALU.max))
        link(V.tensor_tensor(pick, s, top[:, :, i:i + 1].to_broadcast([P, n, E]), ALU.is_equal))
        link(V.tensor_tensor(pick, pick, bcast(rank_row, [P, n, E]), ALU.mult))
        link(V.tensor_reduce(top[:, :, 2:3], pick, AX.X, ALU.max))
        link(V.tensor_tensor(hot, pick, top[:, :, 2:3].to_broadcast([P, n, E]), ALU.is_equal))
        if i == 0:
            link(V.scalar_tensor_tensor(out=s, in0=hot, scalar=-BIG, in1=s, op0=ALU.mult, op1=ALU.add))


SLOPE = 0.2


def graph_phase(nc, counts, apart_total, gat_h, gat_src, att_dst, sums):
    NT = NODES // P
    NC = NODES // G
    T4 = G // P
    H, E = 4, 4
    W = E + 1
    TG = 4
    NG = NT // TG
    R = 4
    with Phase(nc, "graph") as ph:
        cnt = ph.sb("cnt", [P, NT, G])
        e = ph.sb("e", [P, R, H, G])
        ad_rows, low_rows = ph.sb("ad_rows", [P, H, G]), ph.sb("low_rows", [P, H, G])
        diag = ph.sb("diag", [P, H, T4, P])
        ident, ones = ph.sb("ident", [P, P]), ph.sb("ones", [P, P])
        feat = ph.sb("feat", [P, R, H * (H * W) + H * W])
        gat_dst = ph.sb("gat_dst", [P, NT, H])
        adst_row = ph.sb("adst_row", [P, H * E])
        src_hi, src_lo = ph.sb("src_hi", [P, NT, H]), ph.sb("src_lo", [P, NT, H])
        mx, m = ph.sb("mx", [P, H, T4]), ph.sb("m", [P, H, T4])
        agg_sb = ph.sb("agg_sb", [H * W, G])
        zero = ph.sb("zero", [P, 1])
        rows_ps = ph.ps("rows_ps", [P, H, G])
        agg = ph.ps("agg", [P, G])
        back = ph.ps("back", [P, T4, 32])
        S = {n: ph.sem(n) for n in (
            "trash made w_in ready b_added kept cleared mask_done tr_done ad_diag low_diag ad_rows_ps low_rows_ps "
            "ad_ready low_ready relued shifted exped p_ready feat_ready used agg_done agg_out back_done stored "
            "chain turn").split()}
        a_in, b_in = ph.sems("a_in"), ph.sems("b_in")
        block = ph.block()
        tables = [t[:, :].rearrange("(t p c n) w -> p t c (n w)", p=P, t=NT, n=G) for t in counts]
        ef = e[:].rearrange("p r h g -> p r (h g)")
        acc = e[:, 0]
        stage = [e[:, 1], e[:, 2]]
        mask = e[:, 3]

        @block.sync
        def _(sp):
            trash = [counts[t][TRASH:TRASH + P, :] for t in range(2)]
            sp.dma_start(adst_row[:], att_dst.partition_broadcast(P)).then_inc(S["w_in"], 16)
            sp.wait_ge(S["made"], 4)
            sp.dma_start(trash[0], apart_total[:]).then_inc(S["trash"], 16)
            sp.dma_start(trash[1], zero[:]).then_inc(S["trash"], 16)
            sp.wait_ge(S["trash"], 32)
            with sp.Fori(0, NC) as c:
                with sp.Fori(0, NG // 2) as k2:
                    for q in range(2):
                        k = sp.snap(2 * k2 + q)
                        kt = sp.snap(k * TG)
                        sp.wait_ge(S["p_ready"], c * NT)
                        sp.sem_inc(S["turn"], 1)
                        sp.dma_start(cnt[:, bass.ds(kt, TG)], tables[0][:, bass.ds(kt, TG), c]).then_inc(a_in[q], 16)
                        sp.wait_ge(S["used"], c * NT)
                        sp.sem_inc(S["turn"], 1)
                        sp.wait_ge(S["b_added"], c * NG + 2 * k2 + q)
                        sp.sem_inc(S["turn"], 1)
                        sp.dma_start(stage[q], tables[1][:, bass.ds(kt, TG), c]).then_inc(b_in[q], 16)

        @block.gpsimd
        def _(pool):
            identity(nc, pool, ident, S["made"])
            pool.wait_ge(S["made"], 2)
            nc.gpsimd.memset(ones[:], 1.0).then_inc(S["made"], 1)
            pool.wait_ge(S["made"], 3)
            nc.gpsimd.memset(zero[:], 0.0).then_inc(S["made"], 1)
            pool.sem_inc(S["b_added"], 1)
            with pool.Fori(0, NC) as c:
                with pool.Fori(0, NG // 2) as k2:
                    for q in range(2):
                        k = 2 * k2 + q
                        pool.wait_ge(a_in[q], 16 * (c * (NG // 2) + k2 + 1))
                        pool.wait_ge(b_in[q], 16 * (c * (NG // 2) + k2 + 1))
                        part = cnt[:, bass.ds(k * TG, TG)]
                        nc.gpsimd.tensor_tensor(part, part, stage[q], ALU.add).then_inc(S["b_added"], 1)
                pool.wait_ge(S["low_ready"], c + 1)
                pool.sem_inc(S["turn"], 1)
                with pool.Fori(0, NT // R) as k:
                    for r in range(R):
                        pool.wait_ge(S["relued"], c * NT + k * R + r + 1)
                        nc.gpsimd.tensor_tensor(e[:, r], e[:, r], low_rows[:], ALU.add).then_inc(S["shifted"], 1)

        @block.tensor
        def _(pe):
            pe.wait_ge(S["made"], 4)
            with pe.Fori(0, NC) as c:
                pe.wait_ge(S["ad_diag"], c + 1)
                pe.wait_ge(S["low_ready"], c)
                for h in range(H):
                    last = nc.tensor.matmul(rows_ps[:, h], ones[:], diag[:, h].rearrange("p t n -> p (t n)"), start=True, stop=True)
                last.then_inc(S["ad_rows_ps"], 1)
                pe.wait_ge(S["ad_ready"], c + 1)
                pe.wait_ge(S["kept"], H * NT * (c + 1))
                for h in range(H):
                    for t in range(T4):
                        last = nc.tensor.transpose(rows_ps[:, h, t * P:(t + 1) * P], acc[:, h, t * P:(t + 1) * P], ident[:])
                last.then_inc(S["tr_done"], 1)
                pe.wait_ge(S["low_diag"], c + 1)
                for h in range(H):
                    last = nc.tensor.matmul(rows_ps[:, h], ones[:], diag[:, h].rearrange("p t n -> p (t n)"), start=True, stop=True)
                last.then_inc(S["low_rows_ps"], 1)
                pe.wait_ge(S["agg_out"], c)

                def add(n, r, start, stop):
                    pe.wait_ge(S["p_ready"], c * NT + n + 1)
                    pe.wait_ge(S["feat_ready"], c * NT + n + 1)
                    for h in range(H):
                        last = nc.tensor.matmul(agg[0:H * W], feat[:, r, h * H * W:(h + 1) * H * W], e[:, r, h], start=start and h == 0, stop=stop and h == H - 1)
                    last.then_inc(S["used"], 1)

                for r in range(R):
                    add(r, r, r == 0, False)
                with pe.Fori(1, NT // R - 1) as k:
                    for r in range(R):
                        add(k * R + r, r, False, False)
                for r in range(R):
                    add(NT - R + r, r, False, r == R - 1)
                pe.wait_ge(S["agg_out"], c + 1)
                pe.wait_ge(S["stored"], c)
                pe.sem_inc(S["turn"], 1)
                for t in range(T4):
                    last = nc.tensor.transpose(back[:, t, 0:H * W], agg_sb[:, t * P:(t + 1) * P], ident[0:H * W, 0:H * W])
                last.then_inc(S["back_done"], 1)

        @block.scalar
        def _(act):
            with act.Fori(0, NC) as c:
                act.wait_ge(S["ad_rows_ps"], c + 1)
                act.wait_ge(S["relued"], c * NT)
                nc.scalar.activation(ad_rows[:], rows_ps[:], ACT.Copy).then_inc(S["ad_ready"], 1)
                act.wait_ge(S["low_rows_ps"], c + 1)
                act.wait_ge(S["shifted"], c * NT)
                nc.scalar.activation(low_rows[:], rows_ps[:], ACT.Copy).then_inc(S["low_ready"], 1)
                act.wait_ge(S["ad_ready"], c + 1)

                def leaky(n, r, first=False):
                    if not first:
                        act.wait_ge(S["used"], c * NT + n - R + 1)
                    for h in range(H):
                        last = nc.scalar.activation(e[:, r, h], ad_rows[:, h], ACT.Relu, bias=src_hi[:, bass.ds(n, 1), h], scale=1.0 - SLOPE)
                    last.then_inc(S["relued"], 1)

                def expo(n, r):
                    act.wait_ge(S["shifted"], c * NT + n + 1)
                    for h in range(H):
                        last = nc.scalar.activation(e[:, r, h], e[:, r, h], ACT.Exp, bias=src_lo[:, bass.ds(n, 1), h])
                    last.then_inc(S["exped"], 1)

                leaky(0, 0, True)
                leaky(1, 1, True)
                for r in range(2):
                    leaky(r + 2, r + 2, True)
                    expo(r, r)
                with act.Fori(1, NT // R) as k:
                    leaky(k * R, 0)
                    expo(k * R - 2, 2)
                    leaky(k * R + 1, 1)
                    expo(k * R - 1, 3)
                    leaky(k * R + 2, 2)
                    expo(k * R, 0)
                    leaky(k * R + 3, 3)
                    expo(k * R + 1, 1)
                expo(NT - 2, 2)
                expo(NT - 1, 3)

        @block.vector
        def _(dve):
            V = nc.vector
            dve.wait_ge(S["w_in"], 16)
            for t0 in range(0, NT, 4):
                for t in range(t0, t0 + 4):
                    last = V.tensor_tensor(diag[:, 0, 0, (t - t0) * 16:(t - t0 + 1) * 16], gat_h[:, t], adst_row[:], ALU.mult)
                last.then_inc(S["ready"], 1)
                dve.wait_ge(S["ready"], t0 // 2 + 1)
                V.tensor_reduce(gat_dst[:, t0:t0 + 4], diag[:, 0, 0, 0:64].rearrange("p (t h e) -> p t h e", h=H, e=E), AX.X, ALU.add).then_inc(S["ready"], 1)
                dve.wait_ge(S["ready"], t0 // 2 + 2)
            nr = NT // 2
            V.tensor_scalar(src_hi[:], gat_src[:], 1.0 - SLOPE, None, ALU.mult)
            V.tensor_scalar(src_lo[:], gat_src[:], SLOPE, None, ALU.mult)
            V.memset(feat[:], 0.0).then_inc(S["ready"], 1)
            dve.wait_ge(S["ready"], nr + 1)
            fv = feat[:].rearrange("p r (h s) -> p r h s", s=H * W + W)
            V.memset(fv[:, :, :, E:E + 1], 1.0).then_inc(S["ready"], 1)
            dve.wait_ge(S["ready"], nr + 2)
            dve.wait_ge(S["made"], 4)

            def spread(values, sem):
                V.tensor_tensor(diag[:], ident[:].rearrange("p (a b n) -> p a b n", a=1, b=1).to_broadcast([P, H, T4, P]),
                                values.rearrange("p h (t o) -> p h t o", o=1).to_broadcast([P, H, T4, P]), ALU.mult).then_inc(S[sem], 1)

            with dve.Fori(0, NC) as c:
                dve.wait_ge(S["low_rows_ps"], c)
                V.tensor_copy(m[:], gat_dst[:, bass.ds(c * T4, T4)].rearrange("p t h -> p h t")).then_inc(S["cleared"], 1)
                dve.wait_ge(S["cleared"], 2 * c + 1)
                spread(m[:], "ad_diag")
                dve.wait_ge(S["used"], c * NT)
                V.memset(acc, -BIG).then_inc(S["cleared"], 1)
                dve.wait_ge(S["cleared"], 2 * c + 2)
                dve.sem_inc(S["turn"], 1)
                with dve.Fori(0, NG) as k:
                    dve.wait_ge(S["b_added"], c * NG + k + 2)
                    dve.wait_ge(S["kept"], H * (c * NT + k * TG))
                    V.tensor_scalar(mask, cnt[:, bass.ds(k * TG, TG)], 0.0, -BIG, ALU.is_equal, ALU.mult).then_inc(S["mask_done"], 1)
                    dve.wait_ge(S["mask_done"], c * NG + k + 1)
                    for t in range(TG):
                        for h in range(H):
                            if t:
                                dve.wait_ge(S["kept"], H * (c * NT + k * TG) + (H * (t - 1) + h + 1))
                            V.scalar_tensor_tensor(out=acc[:, h], in0=mask[:, t], scalar=gat_src[:, bass.ds(k * TG + t, 1), h], in1=acc[:, h],
                                                   op0=ALU.add, op1=ALU.max).then_inc(S["kept"], 1)
                dve.wait_ge(S["tr_done"], c + 1)
                V.tensor_reduce(mx[:], rows_ps[:].rearrange("p h (t n) -> p h t n", n=P), AX.X, ALU.max).then_inc(S["chain"], 1)
                dve.wait_ge(S["chain"], 4 * c + 1)
                V.tensor_tensor(mx[:], mx[:], m[:], ALU.add).then_inc(S["chain"], 1)
                dve.wait_ge(S["chain"], 4 * c + 2)
                V.scalar_tensor_tensor(out=mx[:], in0=mx[:], scalar=SLOPE, in1=mx[:], op0=ALU.mult, op1=ALU.max).then_inc(S["chain"], 1)
                dve.wait_ge(S["chain"], 4 * c + 3)
                V.scalar_tensor_tensor(out=m[:], in0=m[:], scalar=SLOPE, in1=mx[:], op0=ALU.mult, op1=ALU.subtract).then_inc(S["chain"], 1)
                dve.wait_ge(S["chain"], 4 * c + 4)
                spread(m[:], "low_diag")

                def weigh(n, r):
                    if not (isinstance(n, int) and n < R):
                        dve.wait_ge(S["used"], c * NT + n - R + 1)
                    V.tensor_copy(fv[:, r, 0:H, 0:E], gat_h[:, bass.ds(n, 1)].rearrange("p o (h e) -> p (o h) e", e=E)).then_inc(S["feat_ready"], 1)
                    dve.wait_ge(S["exped"], c * NT + n + 1)
                    V.scalar_tensor_tensor(out=e[:, r], in0=e[:, r], scalar=1.0, in1=cnt[:, bass.ds(n, 1)].to_broadcast([P, H, G]),
                                           op0=ALU.min, op1=ALU.mult).then_inc(S["p_ready"], 1)

                for r in range(R):
                    weigh(r, r)
                with dve.Fori(1, NT // R) as k:
                    for r in range(R):
                        weigh(k * R + r, r)
                dve.wait_ge(S["used"], (c + 1) * NT)
                dve.wait_ge(S["back_done"], c)
                V.tensor_copy(agg_sb[:], agg[0:H * W]).then_inc(S["agg_out"], 1)
                dve.wait_ge(S["back_done"], c + 1)
                V.tensor_copy(sums[:, bass.ds(c * T4, T4)], back[:, :, 0:H * W]).then_inc(S["stored"], 1)
                dve.wait_ge(S["stored"], c + 1)


def scores_phase(nc, sums, b_gat, ln_gamma, ln_beta, gates):
    NT = NODES // P
    H, E, W = 4, 4, 5
    with Phase(nc, "scores") as ph:
        from_row = {n: ph.sb(n, [P, 16]) for n in ("bias", "gamma", "beta")}
        rank_row = ph.sb("rank_row", [P, E])
        A = ph.sb("A", [P, NT, 16])
        B = ph.sb("B", [P, NT, 16])
        rec = ph.sb("rec", [P, NT, H])
        t1, t2, t3 = ph.sb("t1", [P, NT]), ph.sb("t2", [P, NT]), ph.sb("t3", [P, NT])
        s = ph.sb("s", [P, NT, E])
        f1, f2, pick = ph.sb("f1", [P, NT, E]), ph.sb("f2", [P, NT, E]), ph.sb("pick", [P, NT, E])
        top = ph.sb("top", [P, NT, 3])
        w_in, made, asked, rooted, chain = (ph.sem(n) for n in ("w_in", "made", "asked", "rooted", "chain"))
        block = ph.block()

        @block.sync
        def _(sp):
            for n, a in (("bias", b_gat), ("gamma", ln_gamma), ("beta", ln_beta)):
                sp.dma_start(from_row[n][:], a.partition_broadcast(P)).then_inc(w_in, 16)

        @block.scalar
        def _(act):
            act.wait_ge(asked, 1)
            nc.scalar.activation(t2[:], t2[:], ACT.Sqrt).then_inc(rooted, 1)
            act.wait_ge(asked, 2)
            nc.scalar.activation(t1[:], t1[:], ACT.Exp).then_inc(rooted, 1)

        @block.vector
        def _(dve):
            V = nc.vector
            link = Chain(dve, chain)
            for i in range(E):
                last = V.memset(rank_row[:, i:i + 1], float(E - i))
            dve.wait_ge(w_in, 48)
            sv = sums[:].rearrange("p t (h w) -> p t h w", w=W)
            link(V.tensor_scalar(rec[:].rearrange("p t (h o) -> p t h o", o=1), sv[:, :, :, E:W], 1e-16, None, ALU.add))
            link(V.reciprocal(rec[:], rec[:]))
            Av = A[:].rearrange("p t (h e) -> p t h e", e=E)
            link(V.tensor_tensor(Av, sv[:, :, :, 0:E], rec[:].rearrange("p t (h o) -> p t h o", o=1).to_broadcast([P, NT, H, E]), ALU.mult))
            link(V.tensor_tensor(A[:], A[:], bcast(from_row["bias"][:], [P, NT, 16]), ALU.add))
            wide = lambda t: t[:].rearrange("p (t o) -> p t o", o=1)
            link(V.tensor_reduce(t1[:], A[:], AX.X, ALU.add))
            link(V.tensor_scalar(t1[:], t1[:], 1.0 / 16, None, ALU.mult))
            link(V.tensor_tensor(A[:], A[:], wide(t1).to_broadcast([P, NT, 16]), ALU.subtract))
            link(V.tensor_tensor(B[:], A[:], A[:], ALU.mult))
            link(V.tensor_reduce(t2[:], B[:], AX.X, ALU.add))
            V.tensor_scalar(t2[:], t2[:], 1.0 / 16, EPS, ALU.mult, ALU.add).then_inc(asked, 1)
            dve.wait_ge(rooted, 1)
            link(V.reciprocal(t2[:], t2[:]))
            link(V.tensor_tensor(A[:], A[:], wide(t2).to_broadcast([P, NT, 16]), ALU.mult))
            link(V.tensor_tensor(A[:], A[:], bcast(from_row["gamma"][:], [P, NT, 16]), ALU.mult))
            link(V.tensor_tensor(A[:], A[:], bcast(from_row["beta"][:], [P, NT, 16]), ALU.add))
            link(V.tensor_reduce(s[:], A[:].rearrange("p t (h e) -> p t e h", e=E), AX.X, ALU.add))
            link(V.tensor_scalar(s[:], s[:], 1.0 / H, None, ALU.mult))
            best_two(V, link, s[:], f1[:], f2[:], pick[:], top[:], rank_row[:], E)
            V.tensor_tensor(wide(t1), top[:, :, 1:2], top[:, :, 0:1], ALU.subtract).then_inc(asked, 1)
            dve.wait_ge(rooted, 2)
            link(V.tensor_scalar(t2[:], t1[:], 1.0, None, ALU.add))
            link(V.reciprocal(t2[:], t2[:]))
            link(V.tensor_tensor(t3[:], t1[:], t2[:], ALU.mult))
            link(V.tensor_tensor(f1[:], f1[:], wide(t2).to_broadcast([P, NT, E]), ALU.mult))
            link(V.tensor_tensor(f2[:], f2[:], wide(t3).to_broadcast([P, NT, E]), ALU.mult))
            link(V.tensor_tensor(gates[:], f1[:], f2[:], ALU.add))


def experts_phase(nc, name, n_experts, xT, gates, w1, b1, w2, b2, h_in, h_out):
    HID = w1.shape[2]
    MH = HID // P
    T4 = G // P
    NG = NODES // G
    X = n_experts
    with Phase(nc, name) as ph:
        w1_sb = ph.sb("w1_sb", [P, X, KT, HID])
        w2_sb = ph.sb("w2_sb", [P, X, MH, D])
        b1_col = ph.sb("b1_col", [P, X, MH])
        b2_row = ph.sb("b2_row", [P, X, D])
        x = ph.sb("x", [P, 2, KT, G])
        h = ph.sb("h", [P, 2, T4, D])
        hid = ph.sb("hid", [P, 2, MH, G])
        first = ph.ps("first", [P, MH, G])
        second = ph.ps("second", [P, 2, T4, D])
        w_in, first_done, gelu_done, second_done, added, biased = (
            ph.sem(n) for n in ("w_in", "first_done", "gelu_done", "second_done", "added", "biased"))
        x_in, h_in_sem, stored = ph.sems("x_in"), ph.sems("h_in"), ph.sems("stored")
        block = ph.block()
        xv = xT.rearrange("(k p) (g t) -> p k g t", p=P, t=G)
        hv = h_in.rearrange("(g t p) d -> p g t d", p=P, t=T4)
        ov = h_out.rearrange("(g t p) d -> p g t d", p=P, t=T4)
        N_W = 2 * X + 2

        @block.sync
        def _(sp):
            for e in range(X):
                sp.dma_start(w1_sb[:, e], w1[e].rearrange("(k p) n -> p k n", p=P)).then_inc(w_in, 16)
                sp.dma_start(w2_sb[:, e], w2[e].rearrange("(k p) n -> p k n", p=P)).then_inc(w_in, 16)
            with nc.allow_non_contiguous_dma(reason="biases, once"):
                sp.dma_start(b1_col[:], b1.rearrange("e (m p) -> p e m", p=P)).then_inc(w_in, 16)
            sp.dma_start(b2_row[:].rearrange("p e d -> p (e d)"), b2.rearrange("e d -> (e d)").partition_broadcast(P)).then_inc(w_in, 16)
            for q in range(2):
                sp.dma_start(x[:, q], xv[:, :, q]).then_inc(x_in[q], 16)
                sp.dma_start(h[:, q], hv[:, q]).then_inc(h_in_sem[q], 16)
            with sp.Fori(1, NG // 2) as p:
                for q in range(2):
                    g = sp.snap(2 * p + q)
                    sp.wait_ge(first_done, MH * X * (2 * p + q - 1))
                    sp.dma_start(x[:, q], xv[:, :, g]).then_inc(x_in[q], 16)
                    g = sp.snap(2 * p + q)
                    sp.wait_ge(stored[q], 16 * p)
                    sp.dma_start(h[:, q], hv[:, g]).then_inc(h_in_sem[q], 16)

        @block.tensor
        def _(pe):
            pe.wait_ge(w_in, 16 * N_W)

            def hidden(p, q, e, start):
                n = (2 * p + q) * X + e
                if e == 0:
                    pe.wait_ge(x_in[q], 16 * (p + 1))
                for m in range(MH):
                    if not start:
                        pe.wait_ge(gelu_done, MH * n + (m + 1 - MH))
                    for k in range(KT):
                        last = nc.tensor.matmul(first[:, m], w1_sb[:, e, k, m * P:(m + 1) * P], x[:, q, k], start=(k == 0), stop=(k == KT - 1))
                    last.then_inc(first_done, 1)

            def out(p, q, e, start):
                n = (2 * p + q) * X + e
                pe.wait_ge(gelu_done, MH * n + MH)
                if not start:
                    pe.wait_ge(added, n - 1)
                for t in range(T4):
                    for k in range(MH):
                        last = nc.tensor.matmul(second[:, e % 2, t], hid[:, e % 2, k, t * P:(t + 1) * P], w2_sb[:, e, k], start=(k == 0), stop=(k == MH - 1))
                last.then_inc(second_done, 1)

            def group(p, q, start, last):
                for e in range(X):
                    if e + 1 < X:
                        hidden(p, q, e + 1, False)
                    elif not last:
                        hidden(*((p, 1) if q == 0 else (p + 1, 0)), 0, False)
                    out(p, q, e, start and e < 2)

            hidden(0, 0, 0, True)
            group(0, 0, True, False)
            group(0, 1, False, False)
            with pe.Fori(1, NG // 2 - 1) as p:
                for q in range(2):
                    group(p, q, False, False)
            group(NG // 2 - 1, 0, False, False)
            group(NG // 2 - 1, 1, False, True)

        @block.scalar
        def _(act):
            act.wait_ge(w_in, 16 * N_W)

            def gelu(p, q, start):
                for e in range(X):
                    n = (2 * p + q) * X + e
                    for m in range(MH):
                        act.wait_ge(first_done, MH * n + (m + 1))
                        if m == 0 and not (start and e < 2):
                            act.wait_ge(second_done, n - 1)
                        nc.scalar.activation(hid[:, e % 2, m], first[:, m], ACT.Gelu, bias=b1_col[:, e, m:m + 1]).then_inc(gelu_done, 1)

            def store(p, q):
                g = 2 * p + q
                act.wait_ge(added, X * (g + 1))
                act.dma_start(ov[:, g], h[:, q]).then_inc(stored[q], 16)

            gelu(0, 0, True)
            gelu(0, 1, False)
            store(0, 0)
            with act.Fori(1, NG // 2) as p:
                gelu(p, 0, False)
                store(p - 1, 1)
                gelu(p, 1, False)
                store(p, 0)
            store(NG // 2 - 1, 1)
            for q in range(2):
                act.wait_ge(stored[q], 16 * (NG // 2))

        @block.vector
        def _(dve):
            dve.wait_ge(w_in, 16 * N_W)
            with dve.Fori(0, NG // 2) as p:
                for q in range(2):
                    dve.wait_ge(h_in_sem[q], 16 * (p + 1))
                    for e in range(X):
                        n = (2 * p + q) * X + e
                        if e:
                            dve.wait_ge(added, n)
                        gate = lambda t: gates[:, bass.ds((2 * p + q) * T4 + t, 1), e]
                        for t in range(T4):
                            last = nc.vector.scalar_tensor_tensor(out=h[:, q, t], in0=b2_row[:, e], scalar=gate(t), in1=h[:, q, t], op0=ALU.mult, op1=ALU.add)
                        last.then_inc(biased, 1)
                        dve.wait_ge(biased, n + 1)
                        dve.wait_ge(second_done, n + 1)
                        for t in range(T4):
                            last = nc.vector.scalar_tensor_tensor(out=h[:, q, t], in0=second[:, e % 2, t], scalar=gate(t), in1=h[:, q, t], op0=ALU.mult, op1=ALU.add)
                        last.then_inc(added, 1)


class Local:

    def __init__(self, eng, sem):
        self.eng, self.sem, self.n = eng, sem, 0

    def mark(self, instruction):
        instruction.then_inc(self.sem, 1)
        self.n += 1
        return self.n

    def after(self, n):
        self.eng.wait_ge(self.sem, n)

    def link(self, instruction):
        self.after(self.mark(instruction))

    def end(self):
        self.after(self.n)
        self.eng.sem_clear(self.sem)


def attention_phase(nc, h2, qkv_wT, qkv_b, q_gamma, q_beta, k_gamma, k_beta, proj_wT, proj_b, gate_w, h3, x2T, logits):
    N = 256
    NB = NODES // N
    NT = N // P
    NH, HD = 8, 32
    K_VAL = int(N * 0.3)
    ROUNDS = -(-K_VAL // 8)
    SENT = ROUNDS * 8 - K_VAL
    SCALE = HD ** -0.5
    with Phase(nc, "attn") as ph:
        wqkv = ph.sb("wqkv", [P, KT, 3 * D])
        wproj = ph.sb("wproj", [P, KT, D])
        wgate = ph.sb("wgate", [P, KT, 8])
        bias = ph.sb("bias", [P, 3 * D])
        pbias = ph.sb("pbias", [P, D])
        gam, bet = ph.sb("gam", [P, 2, NH, HD]), ph.sb("bet", [P, 2, NH, HD])
        gb = ph.sb("gb", [P, 4, HD])
        eps = ph.sb("eps", [P, 1])
        ident = ph.sb("ident", [P, P])
        h = ph.sb("h", [P, NT, D])
        hb = ph.sb("hb", [P, NT, D])
        xn = ph.sb("xn", [P, NT, D])
        xT = ph.sb("xT", [P, KT, N])
        qk = ph.sb("qk", [P, NT, 2 * D])
        sq = ph.sb("sq", [P, NT, 2 * D])
        vraw = ph.sb("vraw", [P, NT, D])
        v = ph.sb("v", [P, NT, D])
        qkT = ph.sb("qkT", [P, 2, KT, N])
        stats, mv = ph.sb("stats", [P, 2, NT, 6]), ph.sb("mv", [P, 2, NT, 2])
        dev = ph.sb("dev", [P, 2, NT, 3])
        hs = ph.sb("hs", [P, 4, NT * 2 * NH])
        s = ph.sb("s", [P, 4, N + SENT])
        w = ph.sb("w", [P, 4, N + SENT])
        e = ph.sb("e", [P, 4, N])
        p_ = ph.sb("p", [P, 4, N])
        pT = ph.sb("pT", [P, NT, NT, P])
        best = ph.sb("best", [P, 4, 8])
        neg = ph.sb("neg", [P, 4, 1])
        sums = ph.sb("sums", [P, NT, NH])
        rec = ph.sb("rec", [P, NT, NH])
        o, oT = ph.sb("o", [P, NT, D]), ph.sb("oT", [P, KT, N])
        h3_sb, x2 = ph.sb("h3_sb", [P, NT, D]), ph.sb("x2", [P, NT, D])
        x2T_sb = ph.sb("x2T_sb", [P, KT, N])
        s_ps = ph.ps("s_ps", [P, NT, G])
        pt_ps = ph.ps("pt_ps", [P, NT, G])
        pv = ph.ps("pv", [P, NT, D])
        small_ps = ph.ps("small_ps", [P, G])
        big_ps = ph.ps("big_ps", [P, 2 * G])
        S = {n: ph.sem(n) for n in (
            "w_in made rows chain turn h_in var1 std1 xn_ready xn_tr xT_ready qkv_done qk_biased v_taken centre centred "
            "squared var2 std2 rstd pool qk_ready qk_tr qkT_ready v_ready scores_done s_ready neg_ready exp_done picked "
            "p_tr pT_ready pv_done rec_ready o_ready o_tr oT_ready proj_done h3_ready var3 std3 x2_ready x2_tr "
            "x2T_ready stored_h stored_x logits_done logits_saved hb_ready").split()}
        block = ph.block()
        hv = h2.rearrange("(b t p) d -> p b t d", p=P, t=NT)
        ov = h3.rearrange("(b t p) d -> p b t d", p=P, t=NT)
        xv = x2T.rearrange("(k p) (b t) -> p k b t", p=P, t=N)
        by_tok = small_ps[:].rearrange("p (t d) -> p t d", d=D)
        by_dim = small_ps[:].rearrange("p (k t) -> p k t", t=N)
        big_dim = big_ps[:].rearrange("p (a k t) -> p a k t", a=2, t=N)
        N_W = 9
        ITEMS = NT * NH

        def over(body):
            def run(eng):
                body(0, True, False)
                with eng.Fori(1, NB - 1) as b:
                    body(b, False, False)
                body(NB - 1, False, True)
            return run

        @block.sync
        def _(sp):
            for t, a in ((wqkv, qkv_wT), (wproj, proj_wT), (wgate, gate_w)):
                sp.dma_start(t[:], a.rearrange("(k p) n -> p k n", p=P)).then_inc(S["w_in"], 16)
            sp.dma_start(bias[:], qkv_b.partition_broadcast(P)).then_inc(S["w_in"], 16)
            sp.dma_start(pbias[:], proj_b.partition_broadcast(P)).then_inc(S["w_in"], 16)
            for i, a in enumerate((q_gamma, k_gamma, q_beta, k_beta)):
                sp.dma_start(gb[:, i], a.partition_broadcast(P)).then_inc(S["w_in"], 16)
            sp.dma_start(h[:], hv[:, 0]).then_inc(S["h_in"], 16)
            with sp.Fori(1, NB) as b:
                b_ = sp.snap(b)
                sp.wait_ge(S["hb_ready"], b)
                sp.dma_start(h[:], hv[:, b_]).then_inc(S["h_in"], 16)

        @block.gpsimd
        def _(pool):
            identity(nc, pool, ident, S["made"])
            pool.wait_ge(S["made"], 2)
            nc.gpsimd.memset(eps[:], EPS).then_inc(S["made"], 1)
            pool.wait_ge(S["made"], 3)
            pool.wait_ge(S["rows"], 3)

            def norm_heads(b):
                q4 = qk[:].rearrange("p t (n d) -> p (t n) d", d=HD)
                pool.wait_ge(S["centre"], b + 1)
                nc.gpsimd.tensor_tensor(q4, q4, hs[:, 0:1].rearrange("p o n -> p n o").to_broadcast([P, NT * 2 * NH, HD]), ALU.subtract).then_inc(S["centred"], 1)
                pool.wait_ge(S["centred"], b + 1)
                pool.wait_ge(S["squared"], b + 1)
                pool.wait_ge(S["rstd"], b + 1)
                nc.gpsimd.tensor_tensor(q4, q4, hs[:, 3:4].rearrange("p o n -> p n o").to_broadcast([P, NT * 2 * NH, HD]), ALU.mult).then_inc(S["pool"], 1)
                pool.wait_ge(S["pool"], 2 * b + 1)
                nc.gpsimd.tensor_tensor(qk[:], qk[:], bcast(gam[:].rearrange("p a n d -> p (a n d)"), [P, NT, 2 * D]), ALU.mult).then_inc(S["pool"], 1)
                pool.wait_ge(S["pool"], 2 * b + 2)
                nc.gpsimd.tensor_tensor(qk[:], qk[:], bcast(bet[:].rearrange("p a n d -> p (a n d)"), [P, NT, 2 * D]), ALU.add).then_inc(S["qk_ready"], 1)

            def body(b, first, last):
                pool.wait_ge(S["v_taken"], NT * (b + 1))
                if not first:
                    pool.wait_ge(S["pv_done"], ITEMS * b)
                nc.gpsimd.tensor_tensor(v[:], vraw[:], bcast(bias[:, 2 * D:], [P, NT, D]), ALU.add).then_inc(S["v_ready"], 1)
                if not first:
                    pool.wait_ge(S["h3_ready"], b)
                nc.gpsimd.tensor_tensor(hb[:], h[:], bcast(pbias[:], [P, NT, D]), ALU.add).then_inc(S["hb_ready"], 1)
                if not last:
                    norm_heads(b + 1)

            pool.wait_ge(S["w_in"], 16 * N_W)
            norm_heads(0)
            pool.wait_ge(S["xn_ready"], 1)
            over(body)(pool)

        @block.tensor
        def _(pe):
            pe.wait_ge(S["made"], 3)
            pe.wait_ge(S["w_in"], 16 * N_W)

            def xn_turn(b):
                pe.wait_ge(S["xn_ready"], b + 1)
                if not (isinstance(b, int) and b < 2):
                    pe.wait_ge(S["logits_saved"], b - 1)
                for t in range(NT):
                    for k in range(KT):
                        last = nc.tensor.transpose(by_dim[:, k, t * P:(t + 1) * P], xn[:, t, k * P:(k + 1) * P], ident[:])
                last.then_inc(S["xn_tr"], 1)

            def qkv(b, t, first=False):
                if t == 0:
                    pe.wait_ge(S["xT_ready"], b + 1)
                    if not first:
                        pe.wait_ge(S["qkT_ready"], b)
                else:
                    pe.wait_ge(S["qk_biased"], NT * b + t)
                    pe.wait_ge(S["v_taken"], NT * b + t)
                for k in range(KT):
                    nc.tensor.matmul(big_ps[:, 0:2 * D], xT[:, k, t * P:(t + 1) * P], wqkv[:, k, 0:2 * D], start=(k == 0), stop=(k == KT - 1))
                for k in range(KT):
                    last = nc.tensor.matmul(big_ps[:, 2 * D:3 * D], xT[:, k, t * P:(t + 1) * P], wqkv[:, k, 2 * D:], start=(k == 0), stop=(k == KT - 1))
                last.then_inc(S["qkv_done"], 1)

            def qk_turn(b):
                pe.wait_ge(S["qk_ready"], b + 1)
                pe.wait_ge(S["v_taken"], NT * (b + 1))
                for a in range(2):
                    for t in range(NT):
                        for k in range(KT):
                            last = nc.tensor.transpose(big_dim[:, a, k, t * P:(t + 1) * P], qk[:, t, a * D + k * P:a * D + (k + 1) * P], ident[:])
                last.then_inc(S["qk_tr"], 1)

            def scores(b, hh, first=False):
                if hh == 0:
                    pe.wait_ge(S["qkT_ready"], b + 1)
                rows = slice(HD * (hh % 4), HD * (hh % 4) + HD)
                for t in range(NT):
                    n = ITEMS * b + (NT * hh + t)
                    if not (first and hh == 0):
                        pe.wait_ge(S["s_ready"], n - 1)
                    nc.tensor.matmul(s_ps[:, t, 0:N], qkT[rows, 0, hh // 4, t * P:(t + 1) * P], qkT[rows, 1, hh // 4], start=True, stop=True,
                                     tile_position=(HD * (hh % 4), 0)).then_inc(S["scores_done"], 1)

            def values(b, hh, first):
                if hh == 0:
                    pe.wait_ge(S["v_ready"], b + 1)
                    if not first:
                        pe.wait_ge(S["o_ready"], b)
                for t in range(NT):
                    n = ITEMS * b + (NT * hh + t)
                    pe.wait_ge(S["picked"], n + 1)
                    if not (first and hh == 0):
                        pe.wait_ge(S["pT_ready"], n - 1)
                    for m in range(NT):
                        last = nc.tensor.transpose(pt_ps[:, t, m * P:(m + 1) * P], p_[:, 2 * (hh % 2) + t, m * P:(m + 1) * P], ident[:])
                    last.then_inc(S["p_tr"], 1)
                for t in range(NT):
                    n = ITEMS * b + (NT * hh + t)
                    pe.wait_ge(S["pT_ready"], n + 1)
                    for m in range(NT):
                        last = nc.tensor.matmul(pv[:, t, hh * HD:(hh + 1) * HD], pT[:, t, m], v[:, m, hh * HD:(hh + 1) * HD], start=(m == 0), stop=(m == NT - 1))
                    last.then_inc(S["pv_done"], 1)

            def o_turn(b):
                pe.wait_ge(S["o_ready"], b + 1)
                pe.wait_ge(S["xT_ready"], b + 1)
                for t in range(NT):
                    for k in range(KT):
                        last = nc.tensor.transpose(by_dim[:, k, t * P:(t + 1) * P], o[:, t, k * P:(k + 1) * P], ident[:])
                last.then_inc(S["o_tr"], 1)
                pe.wait_ge(S["oT_ready"], b + 1)
                for t in range(NT):
                    for k in range(KT):
                        last = nc.tensor.matmul(by_tok[:, t], oT[:, k, t * P:(t + 1) * P], wproj[:, k], start=(k == 0), stop=(k == KT - 1))
                last.then_inc(S["proj_done"], 1)

            def x2_turn(b):
                pe.wait_ge(S["x2_ready"], b + 1)
                for t in range(NT):
                    for k in range(KT):
                        last = nc.tensor.transpose(by_dim[:, k, t * P:(t + 1) * P], x2[:, t, k * P:(k + 1) * P], ident[:])
                last.then_inc(S["x2_tr"], 1)
                pe.wait_ge(S["x2T_ready"], b + 1)
                for t in range(NT):
                    for k in range(KT):
                        last = nc.tensor.matmul(by_tok[:, t, 0:8], x2T_sb[:, k, t * P:(t + 1) * P], wgate[:, k], start=(k == 0), stop=(k == KT - 1))
                last.then_inc(S["logits_done"], 1)

            def prepare(b):
                xn_turn(b)
                for t in range(NT):
                    qkv(b, t, True)
                qk_turn(b)

            def body(b, first, last):
                for hh in range(NH):
                    if hh + 1 < NH:
                        scores(b, hh + 1, first)
                    if hh:
                        values(b, hh - 1, first)
                    elif not first:
                        values(b - 1, NH - 1, False)
                    if not first:
                        if hh == 1:
                            o_turn(b - 1)
                        if hh == 2:
                            x2_turn(b - 1)
                    if not last:
                        if hh == 4:
                            xn_turn(b + 1)
                        if hh == 5:
                            qkv(b + 1, 0)
                            qkv(b + 1, 1)
                        if hh == 7:
                            qk_turn(b + 1)
                            scores(b + 1, 0)

            prepare(0)
            scores(0, 0, True)
            over(body)(pe)
            values(NB - 1, NH - 1, False)
            o_turn(NB - 1)
            x2_turn(NB - 1)

        @block.scalar
        def _(act):
            A = nc.scalar.activation

            def xn_std(b):
                act.wait_ge(S["var1"], b + 1)
                A(dev[:, 0, :, 1], dev[:, 0, :, 0], ACT.Sqrt).then_inc(S["std1"], 1)

            def xT_out(b):
                act.wait_ge(S["xn_tr"], b + 1)
                if not (isinstance(b, int) and b == 0):
                    act.wait_ge(S["qkv_done"], NT * b)
                A(xT[:], by_dim, ACT.Copy).then_inc(S["xT_ready"], 1)

            def take_v(b, t):
                act.wait_ge(S["qkv_done"], NT * b + t + 1)
                if t == 0 and not (isinstance(b, int) and b == 0):
                    act.wait_ge(S["v_ready"], b)
                act.wait_ge(S["qk_biased"], NT * b + t + 1)
                A(vraw[:, t], big_ps[:, 2 * D:3 * D], ACT.Copy).then_inc(S["v_taken"], 1)

            def heads_square(b):
                act.wait_ge(S["centred"], b + 1)
                A(sq[:], qk[:], ACT.Square).then_inc(S["squared"], 1)

            def heads_std(b):
                act.wait_ge(S["var2"], b + 1)
                A(hs[:, 2], hs[:, 1], ACT.Sqrt, scale=1.0 / HD, bias=eps[:, 0:1]).then_inc(S["std2"], 1)

            def qkT_out(b, first=False):
                act.wait_ge(S["qk_tr"], b + 1)
                if not first:
                    act.wait_ge(S["scores_done"], ITEMS * b)
                A(qkT[:], big_dim, ACT.Copy).then_inc(S["qkT_ready"], 1)

            def take_scores(b, hh, first):
                for t in range(NT):
                    n = ITEMS * b + (NT * hh + t)
                    act.wait_ge(S["scores_done"], n + 1)
                    if not (first and hh < 2):
                        act.wait_ge(S["picked"], n - 3)
                    A(s[:, 2 * (hh % 2) + t, 0:N], s_ps[:, t, 0:N], ACT.Copy, scale=SCALE).then_inc(S["s_ready"], 1)

            def exps(b, hh):
                for t in range(NT):
                    n = ITEMS * b + (NT * hh + t)
                    act.wait_ge(S["neg_ready"], n + 1)
                    sl = 2 * (hh % 2) + t
                    A(e[:, sl], s[:, sl, 0:N], ACT.Exp, bias=neg[:, sl]).then_inc(S["exp_done"], 1)

            def pT_out(b, hh, first=False):
                for t in range(NT):
                    n = ITEMS * b + (NT * hh + t)
                    act.wait_ge(S["p_tr"], n + 1)
                    if not first:
                        act.wait_ge(S["pv_done"], n - 1)
                    A(pT[:, t].rearrange("p m n -> p (m n)"), pt_ps[:, t, 0:N], ACT.Copy).then_inc(S["pT_ready"], 1)

            def oT_out(b):
                act.wait_ge(S["o_tr"], b + 1)
                A(oT[:], by_dim, ACT.Copy).then_inc(S["oT_ready"], 1)

            def h3_std(b):
                act.wait_ge(S["var3"], b + 1)
                A(dev[:, 1, :, 1], dev[:, 1, :, 0], ACT.Sqrt).then_inc(S["std3"], 1)
                act.dma_start(ov[:, b], h3_sb[:]).then_inc(S["stored_h"], 16)

            def x2T_out(b):
                act.wait_ge(S["x2_tr"], b + 1)
                act.wait_ge(S["stored_x"], 16 * b)
                A(x2T_sb[:], by_dim, ACT.Copy).then_inc(S["x2T_ready"], 1)
                act.wait_ge(S["x2T_ready"], b + 1)
                act.dma_start(xv[:, :, b], x2T_sb[:]).then_inc(S["stored_x"], 16)

            def body(b, first, last):
                for hh in range(NH):
                    if hh + 1 < NH:
                        take_scores(b, hh + 1, first)
                    exps(b, hh)
                    if hh:
                        pT_out(b, hh - 1, first and hh == 1)
                    elif not first:
                        pT_out(b - 1, NH - 1)
                    if not first:
                        if hh == 1:
                            oT_out(b - 1)
                        if hh == 2:
                            h3_std(b - 1)
                            x2T_out(b - 1)
                    if not last:
                        if hh == 4:
                            xn_std(b + 1)
                            xT_out(b + 1)
                        if hh == 5:
                            for t in range(NT):
                                take_v(b + 1, t)
                        if hh == 6:
                            heads_square(b + 1)
                            heads_std(b + 1)
                        if hh == 7:
                            qkT_out(b + 1)
                            take_scores(b + 1, 0, False)

            act.wait_ge(S["made"], 3)
            xn_std(0)
            xT_out(0)
            for t in range(NT):
                take_v(0, t)
            heads_square(0)
            heads_std(0)
            qkT_out(0, True)
            take_scores(0, 0, True)
            over(body)(act)
            pT_out(NB - 1, NH - 1)
            oT_out(NB - 1)
            h3_std(NB - 1)
            x2T_out(NB - 1)
            act.wait_ge(S["stored_h"], 16 * NB)
            act.wait_ge(S["stored_x"], 16 * NB)

        @block.vector
        def _(dve):
            V = nc.vector
            dve.wait_ge(S["w_in"], 16 * N_W)
            for i in range(2):
                V.tensor_copy(gam[:, i], bcast(gb[:, i], [P, NH, HD]))
                last = V.tensor_copy(bet[:, i], bcast(gb[:, 2 + i], [P, NH, HD]))
            last.then_inc(S["rows"], 1)
            for sl in range(4):
                last = V.memset(s[:, sl, N:], BIG)
            last.then_inc(S["rows"], 1)
            dve.wait_ge(S["rows"], 2)
            V.memset(neg[:], 0.0).then_inc(S["rows"], 1)
            dve.wait_ge(S["rows"], 3)

            def moments(loc, x, i, sem):
                for t in range(NT):
                    last = V.bn_stats(stats[:, i, t], x[:, t])
                loc.link(last)
                for t in range(NT):
                    last = V.bn_aggr(mv[:, i, t], stats[:, i, t])
                loc.link(last)
                V.tensor_scalar(dev[:, i, :, 0], mv[:, i, :, 1], EPS, None, ALU.add).then_inc(S[sem], 1)

            def normed(loc, out, x, i, sem, b, done):
                dve.wait_ge(S[sem], b + 1)
                loc.link(V.reciprocal(dev[:, i, :, 2], dev[:, i, :, 1]))
                for t in range(NT):
                    last = V.tensor_scalar(out[:, t], x[:, t], mv[:, i, t, 0:1], dev[:, i, t, 2:3], ALU.subtract, ALU.mult)
                last.then_inc(S[done], 1)

            def x_moments(loc, b):
                dve.wait_ge(S["h_in"], 16 * (b + 1))
                dve.sem_inc(S["turn"], 1)
                moments(loc, h, 0, "var1")

            def x_norm(loc, b):
                normed(loc, xn, h, 0, "std1", b, "xn_ready")

            def qk_bias(loc, b, t):
                dve.wait_ge(S["qkv_done"], NT * b + t + 1)
                V.tensor_tensor(qk[:, t], big_ps[:, 0:2 * D], bias[:, 0:2 * D], ALU.add).then_inc(S["qk_biased"], 1)

            def heads_mean(loc, b):
                dve.wait_ge(S["qk_biased"], NT * (b + 1))
                loc.link(V.tensor_reduce(hs[:, 0], qk[:].rearrange("p t (n d) -> p (t n) d", d=HD), AX.X, ALU.add))
                V.tensor_scalar(hs[:, 0], hs[:, 0], 1.0 / HD, None, ALU.mult).then_inc(S["centre"], 1)

            def heads_var(loc, b):
                dve.wait_ge(S["squared"], b + 1)
                V.tensor_reduce(hs[:, 1], sq[:].rearrange("p t (n d) -> p (t n) d", d=HD), AX.X, ALU.add).then_inc(S["var2"], 1)

            def heads_rstd(loc, b):
                dve.wait_ge(S["std2"], b + 1)
                V.reciprocal(hs[:, 3], hs[:, 2]).then_inc(S["rstd"], 1)

            def o_out(loc, b):
                dve.wait_ge(S["pv_done"], ITEMS * (b + 1))
                dve.wait_ge(S["rec_ready"], b + 1)
                V.tensor_tensor(o[:].rearrange("p t (n d) -> p (t n) d", d=HD), pv[:].rearrange("p t (n d) -> p (t n) d", d=HD),
                                rec[:].rearrange("p t (n o) -> p (t n) o", o=1).to_broadcast([P, ITEMS, HD]), ALU.mult).then_inc(S["o_ready"], 1)

            def h3_out(loc, b):
                dve.wait_ge(S["proj_done"], b + 1)
                dve.wait_ge(S["hb_ready"], b + 1)
                dve.wait_ge(S["stored_h"], 16 * b)
                V.tensor_tensor(h3_sb[:], by_tok, hb[:], ALU.add).then_inc(S["h3_ready"], 1)
                dve.wait_ge(S["h3_ready"], b + 1)
                dve.sem_inc(S["turn"], 1)
                moments(loc, h3_sb, 1, "var3")

            def x2_out(loc, b):
                normed(loc, x2, h3_sb, 1, "std3", b, "x2_ready")

            def logits_out(loc, b):
                dve.wait_ge(S["logits_done"], b + 1)
                V.tensor_copy(logits[:, bass.ds(b * NT, NT), :], by_tok[:, :, 0:8]).then_inc(S["logits_saved"], 1)

            def body(b, first, last):
                loc = Local(dve, S["chain"])
                steps = {}
                if not first:
                    steps.update({(1, 2): (o_out, b - 1), (2, 0): (h3_out, b - 1), (2, 3): (x2_out, b - 1), (3, 0): (logits_out, b - 1)})
                if not last:
                    steps.update({(4, 0): (x_moments, b + 1), (4, 4): (x_norm, b + 1), (5, 2): (qk_bias, b + 1, 0), (5, 6): (qk_bias, b + 1, 1),
                                  (6, 0): (heads_mean, b + 1), (6, 5): (heads_var, b + 1), (6, 8): (heads_rstd, b + 1)})
                for hh in range(NH):
                    replaced = [None, None]
                    for r in range(ROUNDS):
                        if (hh, r) in steps:
                            f, *args = steps[hh, r]
                            f(loc, *args)
                        found = [None, None]
                        for t in range(NT):
                            n = ITEMS * b + (NT * hh + t)
                            sl = 2 * (hh % 2) + t
                            if r == 0:
                                dve.wait_ge(S["s_ready"], n + 1)
                                dve.sem_inc(S["turn"], 1)
                            else:
                                loc.after(replaced[t])
                            found[t] = loc.mark(V.max(best[:, sl], (s if r == 0 else w)[:, sl]))
                        for t in range(NT):
                            sl = 2 * (hh % 2) + t
                            loc.after(found[t])
                            if r == 0:
                                V.tensor_scalar(neg[:, sl], best[:, sl, SENT:SENT + 1], -1.0, None, ALU.mult).then_inc(S["neg_ready"], 1)
                            replaced[t] = loc.mark(V.match_replace(w[:, sl], best[:, sl], (s if r == 0 else w)[:, sl], -BIG))
                    for t in range(NT):
                        n = ITEMS * b + (NT * hh + t)
                        sl = 2 * (hh % 2) + t
                        loc.after(replaced[t])
                        dve.wait_ge(S["exp_done"], n + 1)
                        if not (first and hh < 2):
                            dve.wait_ge(S["p_tr"], n - 3)
                        V.scalar_tensor_tensor(out=p_[:, sl], in0=w[:, sl, 0:N], scalar=-1e38, in1=e[:, sl], op0=ALU.is_lt, op1=ALU.mult,
                                               accum_out=sums[:, t, hh:hh + 1]).then_inc(S["picked"], 1)
                dve.wait_ge(S["picked"], ITEMS * (b + 1))
                V.reciprocal(rec[:], sums[:]).then_inc(S["rec_ready"], 1)
                loc.end()

            loc = Local(dve, S["chain"])
            x_moments(loc, 0)
            x_norm(loc, 0)
            for t in range(NT):
                qk_bias(loc, 0, t)
            heads_mean(loc, 0)
            heads_var(loc, 0)
            heads_rstd(loc, 0)
            loc.end()
            over(body)(dve)
            loc = Local(dve, S["chain"])
            o_out(loc, NB - 1)
            h3_out(loc, NB - 1)
            x2_out(loc, NB - 1)
            logits_out(loc, NB - 1)
            dve.wait_ge(S["logits_saved"], NB)
            loc.end()


def gates_phase(nc, logits, gate_b, gates):
    NT, E = NODES // P, 8
    with Phase(nc, "gates") as ph:
        b_row, rank_row = ph.sb("b_row", [P, E]), ph.sb("rank_row", [P, E])
        s = ph.sb("s", [P, NT, E])
        f1, f2, pick = ph.sb("f1", [P, NT, E]), ph.sb("f2", [P, NT, E]), ph.sb("pick", [P, NT, E])
        t1 = ph.sb("t1", [P, NT])
        top = ph.sb("top", [P, NT, 3])
        w_in, asked, exped, chain = (ph.sem(n) for n in ("w_in", "asked", "exped", "chain"))
        block = ph.block()

        @block.sync
        def _(sp):
            sp.dma_start(b_row[:], gate_b.partition_broadcast(P)).then_inc(w_in, 16)

        @block.scalar
        def _(act):
            act.wait_ge(asked, 1)
            nc.scalar.activation(s[:], s[:], ACT.Exp).then_inc(exped, 1)

        @block.vector
        def _(dve):
            V = nc.vector
            link = Chain(dve, chain)
            for i in range(E):
                V.memset(rank_row[:, i:i + 1], float(E - i))
            wide = lambda t: t[:].rearrange("p (t o) -> p t o", o=1).to_broadcast([P, NT, E])
            dve.wait_ge(w_in, 16)
            link(V.tensor_tensor(s[:], logits[:], bcast(b_row[:], [P, NT, E]), ALU.add))
            link(V.tensor_reduce(t1[:], s[:], AX.X, ALU.max))
            V.tensor_tensor(s[:], s[:], wide(t1), ALU.subtract).then_inc(asked, 1)
            dve.wait_ge(exped, 1)
            link(V.tensor_reduce(t1[:], s[:], AX.X, ALU.add))
            link(V.reciprocal(t1[:], t1[:]))
            link(V.tensor_tensor(s[:], s[:], wide(t1), ALU.mult))
            link(V.tensor_copy(gates[:], s[:]))
            best_two(V, link, s[:], f1[:], f2[:], pick[:], top[:], rank_row[:], E)
            link(V.tensor_tensor(f1[:], f1[:], f2[:], ALU.add))
            link(V.tensor_tensor(gates[:], gates[:], f1[:], ALU.mult))


def audio_tower(nc, x, tok_a_log, tok_d, tok_w_dbc, tok_w_dt, tok_b_dt, lam_re, lam_im, s5_b, s5_c, s5_d, log_step,
                w_gat, att_src, att_dst, b_gat, ln_gamma, ln_beta, gw1, gb1, gw2, gb2, edges_row, edges_col,
                qkv_w, qkv_b, q_gamma, q_beta, k_gamma, k_beta, proj_w, proj_b, gate_w, gate_b, fw1, fb1, fw2, fb2, out):
    def dram(name, shape, dt=F32):
        return nc.dram_tensor(name, shape, dt).ap()

    n_edges = edges_row.shape[1] * edges_row.shape[2]
    n_tiles = n_edges // P
    codes = dram("codes", (CODE_BITS, n_edges), BF16)
    counts = [dram(f"counts{t}", (NODES * NODES, 1)) for t in range(2)]
    nt = NODES // P
    h1, h2, h3 = (dram(f"h{i}", (NODES, D)) for i in (1, 2, 3))
    zT, x2T = dram("zT", (D, NODES)), dram("x2T", (D, NODES))
    with nc.sbuf_tensor("gat_h", [P, nt, 16], F32) as gat_h, nc.sbuf_tensor("gat_src", [P, nt, 4], F32) as gat_src, \
            nc.sbuf_tensor("apart_total", [P, 1], F32) as apart_total, nc.sbuf_tensor("gates0", [P, nt, 4], F32) as gates0, \
            nc.sbuf_tensor("sums", [P, nt, 20], F32) as sums:
        with nc.sbuf_tensor("key_cols", [P, n_tiles], I32) as key_cols:
            edge_phase(nc, edges_row, edges_col, codes, counts, key_cols, apart_total)
            source, tile0 = x, 0
            n_layers = tok_a_log.shape[0]
            for layer in range(n_layers):
                tokens = x.shape[1] >> layer
                seq = 1024 >> layer
                pool_out = layer < n_layers - 1
                target = dram(f"tokens{layer}", (D, tokens // 2 if pool_out else tokens))
                deltaT, uT = dram(f"deltaT{layer}", (D, tokens)), dram(f"uT{layer}", (D, tokens))
                bc_parts = dram(f"bc_parts{layer}", (96, 4 * tokens), BF16)
                project_phase(nc, f"proj{layer}", tokens, source, tok_w_dbc, tok_w_dt, tok_b_dt, layer, deltaT, uT, bc_parts)
                rounds = 1 if pool_out else 2
                scan_phase(nc, f"scan{layer}", tokens, seq, source, deltaT, uT, bc_parts, tok_a_log, tok_d, layer, target, pool_out,
                           codes, counts, key_cols, apart_total, tile0, rounds)
                tile0 += tokens // G * (NS // 4) * rounds * 4
                source = target
            assert tile0 == n_tiles
        mix_phase(nc, source, lam_re, lam_im, log_step, s5_b, s5_c, s5_d, w_gat, att_src, h1, zT, gat_h, gat_src)
        graph_phase(nc, counts, apart_total, gat_h, gat_src, att_dst, sums)
        scores_phase(nc, sums, b_gat, ln_gamma, ln_beta, gates0)
        experts_phase(nc, "experts0", 4, zT, gates0, gw1, gb1, gw2, gb2, h1, h2)
    with nc.sbuf_tensor("logits", [P, nt, 8], F32) as logits, nc.sbuf_tensor("gates1", [P, nt, 8], F32) as gates1:
        attention_phase(nc, h2, qkv_w, qkv_b, q_gamma, q_beta, k_gamma, k_beta, proj_w, proj_b, gate_w, h3, x2T, logits)
        gates_phase(nc, logits, gate_b, gates1)
        experts_phase(nc, "experts1", 8, x2T, gates1, fw1, fb1, fw2, fb2, h3, out)


def kernel(**inputs):
    import numpy as _np
    import concourse.bacc as _bacc
    from concourse import mybir as _mybir
    from concourse.bass_utils import run_bass_kernel_spmd as _run

    i = {name: _np.asarray(a) for name, a in inputs.items()}
    x = i["x"]
    edges = i["L0_ffn_edge_index"]
    laid_out = {
        "x": x.reshape(-1, x.shape[2]).T,
        "tok_a_log": i["L0_tok_A_log"], "tok_d": i["L0_tok_D"],
        "tok_w_dbc": i["L0_tok_W_dbc"].transpose(0, 2, 1), "tok_w_dt": i["L0_tok_W_dt"][:, :, 0], "tok_b_dt": i["L0_tok_b_dt"],
        "lam_re": i["L0_attn_Lambda_re"], "lam_im": i["L0_attn_Lambda_im"],
        "s5_b": i["L0_attn_B"].transpose(2, 1, 0), "s5_c": i["L0_attn_C"].transpose(2, 1, 0),
        "s5_d": i["L0_attn_D"], "log_step": i["L0_attn_log_step"][:, 0],
        "w_gat": i["L0_ffn_W_gat"], "att_src": i["L0_ffn_att_src"].reshape(-1), "att_dst": i["L0_ffn_att_dst"].reshape(-1),
        "b_gat": i["L0_ffn_b_gat"], "ln_gamma": i["L0_ffn_ln_gamma"], "ln_beta": i["L0_ffn_ln_beta"],
        "gw1": i["L0_ffn_W1"], "gb1": i["L0_ffn_b1"], "gw2": i["L0_ffn_W2"], "gb2": i["L0_ffn_b2"],
        "edges_row": edges.reshape(2, 128, -1), "edges_col": edges.reshape(2, -1, 128).transpose(0, 2, 1),
        "qkv_w": i["L1_attn_qkv_w"].T, "qkv_b": i["L1_attn_qkv_b"],
        "q_gamma": i["L1_attn_q_gamma"], "q_beta": i["L1_attn_q_beta"],
        "k_gamma": i["L1_attn_k_gamma"], "k_beta": i["L1_attn_k_beta"],
        "proj_w": i["L1_attn_proj_w"].T, "proj_b": i["L1_attn_proj_b"],
        "gate_w": i["L1_ffn_gate_w"], "gate_b": i["L1_ffn_gate_b"],
        "fw1": i["L1_ffn_W1"], "fb1": i["L1_ffn_b1"], "fw2": i["L1_ffn_W2"], "fb2": i["L1_ffn_b2"],
    }
    nc = _bacc.Bacc("TRN2", target_bir_lowering=False, num_devices=1)
    arrays, args = {}, []
    for name, a in laid_out.items():
        a = _np.ascontiguousarray(a)
        arrays[f"in_{name}"] = a
        args.append(nc.dram_tensor(f"in_{name}", a.shape, _mybir.dt.from_np(a.dtype), kind="ExternalInput").ap())
    args.append(nc.dram_tensor("out_0", (NODES, D), F32, kind="ExternalOutput").ap())
    audio_tower(nc, *args)
    r = _run(nc, [arrays], core_ids=[0])
    return r.results[0]["out_0"].reshape(32, 256, 256)
```
